# Optimizing a Trainium2 kernel written in Bass

```python
import numpy as np
import jax
import jax.numpy as jnp

def _softmax(x, axis=-1):
    return jax.nn.softmax(x, axis=axis)

def _gelu(x):
    return jax.nn.gelu(x, approximate=True)

def _silu(x):
    return jax.nn.silu(x)

def _sigmoid(x):
    return jax.nn.sigmoid(x)

def _layernorm(x, axis=-1, eps=1e-05):
    m = jnp.mean(x, axis=axis, keepdims=True)
    v = jnp.var(x, axis=axis, keepdims=True)
    return (x - m) / jnp.sqrt(v + eps)

def _scatter_add(tgt, idx, src, axis=0):
    return tgt.at[idx].add(src)

def _segment_sum(src, seg, n):
    return jax.ops.segment_sum(src, seg, n)
kernel_name = 'mk_recurrent_d2_jaxref_r8_1112e0'

def setup_inputs(seed: int=0):
    np.random.seed(seed)
    _w = jnp.asarray

    def _L0_attn_setup():
        import jax, jax.numpy as jnp
        import numpy as np
        DIM = 128
        B, N = (8, 512)
        EPS = 1e-06
        key = jax.random.key(seed)
        k1, k2, k3, k4 = jax.random.split(key, 4)
        x = jax.random.normal(k1, (B, N, DIM), dtype=jnp.float32)
        s = 1.0 / np.sqrt(DIM)
        W_qkv = jax.random.uniform(k2, (3 * DIM, DIM), jnp.float32, -s, s)
        W_out = jax.random.uniform(k3, (DIM, DIM), jnp.float32, -s, s)
        b_out = jax.random.uniform(k4, (DIM,), jnp.float32, -s, s)
        return {'x': x, 'W_qkv': W_qkv, 'W_out': W_out, 'b_out': b_out}
    _L0_attn_in = _L0_attn_setup()

    def _L0_ffn_setup():
        import jax, jax.numpy as jnp
        import numpy as np
        NUM_EXPERTS = 8
        TOP_K = 2
        D_MODEL = 128
        EXPERT_CAP = 64
        B, S = (4, 256)
        key = jax.random.key(seed)
        ks = jax.random.split(key, 4)
        scale = 1.0 / np.sqrt(D_MODEL)
        x = jax.random.normal(ks[0], (B, S, D_MODEL), dtype=jnp.float32)
        gate_w = jax.random.normal(ks[1], (D_MODEL, NUM_EXPERTS), dtype=jnp.float32) * scale
        w1 = jax.random.normal(ks[2], (NUM_EXPERTS, D_MODEL, EXPERT_CAP), dtype=jnp.float32) * scale
        b1 = jnp.zeros((NUM_EXPERTS, EXPERT_CAP), dtype=jnp.float32)
        w2 = jax.random.normal(ks[3], (NUM_EXPERTS, EXPERT_CAP, D_MODEL), dtype=jnp.float32) * (1.0 / np.sqrt(EXPERT_CAP))
        b2 = jnp.zeros((NUM_EXPERTS, D_MODEL), dtype=jnp.float32)
        return {'x': x, 'gate_w': gate_w, 'w1': w1, 'b1': b1, 'w2': w2, 'b2': b2}
    _L0_ffn_in = _L0_ffn_setup()

    def _L1_attn_setup():
        import jax, jax.numpy as jnp
        import numpy as np
        B, S, D_IN, D_H = (8, 256, 128, 128)
        LR = 0.01
        key = jax.random.key(seed)
        ks = jax.random.split(key, 6)
        return {'in_seq': jax.random.normal(ks[0], (B, S, D_IN), jnp.float32), 'theta_K': jax.random.normal(ks[1], (D_H, D_IN), jnp.float32) * 0.02, 'theta_V': jax.random.normal(ks[2], (D_H, D_IN), jnp.float32) * 0.02, 'theta_Q': jax.random.normal(ks[3], (D_H, D_IN), jnp.float32) * 0.02, 'W0': jax.random.normal(ks[4], (D_H, D_H), jnp.float32) * 0.02, 'b0': jnp.zeros((D_H,), jnp.float32)}
    _L1_attn_in = _L1_attn_setup()

    def _L1_ffn_setup():
        import jax, jax.numpy as jnp
        import numpy as np
        B, S, D = (4, 256, 128)
        F = 512
        E = 8
        K = 2
        EPS = 1e-09
        key = jax.random.key(seed)
        ks = jax.random.split(key, 6)
        scale = 0.02
        return {'x': jax.random.normal(ks[0], (B, S, D), dtype=jnp.float32), 'Wg': jax.random.normal(ks[1], (D, E), dtype=jnp.float32) * scale, 'W1': jax.random.normal(ks[2], (E, D, F), dtype=jnp.float32) * scale, 'b1': jnp.zeros((E, F), dtype=jnp.float32), 'W2': jax.random.normal(ks[3], (E, F, D), dtype=jnp.float32) * scale, 'b2': jnp.zeros((E, D), dtype=jnp.float32)}
    _L1_ffn_in = _L1_ffn_setup()
    _d = {'L0_attn_x': _L0_attn_in['x'], 'L0_attn_W_qkv': _L0_attn_in['W_qkv'], 'L0_attn_W_out': _L0_attn_in['W_out'], 'L0_attn_b_out': _L0_attn_in['b_out'], 'L0_ffn_gate_w': _L0_ffn_in['gate_w'], 'L0_ffn_w1': _L0_ffn_in['w1'], 'L0_ffn_b1': _L0_ffn_in['b1'], 'L0_ffn_w2': _L0_ffn_in['w2'], 'L0_ffn_b2': _L0_ffn_in['b2'], 'L1_attn_theta_K': _L1_attn_in['theta_K'], 'L1_attn_theta_V': _L1_attn_in['theta_V'], 'L1_attn_theta_Q': _L1_attn_in['theta_Q'], 'L1_attn_W0': _L1_attn_in['W0'], 'L1_attn_b0': _L1_attn_in['b0'], 'L1_ffn_Wg': _L1_ffn_in['Wg'], 'L1_ffn_W1': _L1_ffn_in['W1'], 'L1_ffn_b1': _L1_ffn_in['b1'], 'L1_ffn_W2': _L1_ffn_in['W2'], 'L1_ffn_b2': _L1_ffn_in['b2']}
    _x0 = _d['L0_attn_x']
    _d['L0_attn_x'] = jax.random.normal(jax.random.fold_in(jax.random.key(seed), 1), (16, 256, 128), dtype=_x0.dtype)
    del _x0
    return _d

def reference(L0_attn_x, L0_attn_W_qkv, L0_attn_W_out, L0_attn_b_out, L0_ffn_gate_w, L0_ffn_w1, L0_ffn_b1, L0_ffn_w2, L0_ffn_b2, L1_attn_theta_K, L1_attn_theta_V, L1_attn_theta_Q, L1_attn_W0, L1_attn_b0, L1_ffn_Wg, L1_ffn_W1, L1_ffn_b1, L1_ffn_W2, L1_ffn_b2):

    def _L0_attn_ref(x, W_qkv, W_out, b_out):
        import jax, jax.numpy as jnp
        import numpy as np
        DIM = 128
        B, N = (8, 512)
        EPS = 1e-06
        qkv = jnp.einsum('bnd,ed->bne', x, W_qkv)
        q, k, v = jnp.split(qkv, 3, axis=-1)
        q = jax.nn.relu(q) + EPS
        k = jax.nn.relu(k) + EPS
        kv = jnp.einsum('bnd,bne->bde', k, v)
        z = 1.0 / (jnp.einsum('bnd,bd->bn', q, k.sum(axis=1)) + EPS)
        attn = jnp.einsum('bnd,bde,bn->bne', q, kv, z)
        return jnp.einsum('bne,fe->bnf', attn, W_out) + b_out

    def _L0_ffn_ref(x, gate_w, w1, b1, w2, b2):
        import jax, jax.numpy as jnp
        import numpy as np
        NUM_EXPERTS = 8
        TOP_K = 2
        D_MODEL = 128
        EXPERT_CAP = 64
        B, S = (4, 256)
        Bx, Sx, D = x.shape
        xt = x.reshape(-1, D)
        gates = jax.nn.softmax(xt @ gate_w, axis=-1)
        topk_g, topk_i = jax.lax.top_k(gates, TOP_K)
        tok_w = topk_g.sum(axis=-1)
        sel = (topk_i[:, :, None] == jnp.arange(NUM_EXPERTS)[None, None, :]).any(axis=1)
        h = jax.nn.gelu(jnp.einsum('nd,edh->enh', xt, w1) + b1[:, None, :], approximate=False)
        y = jnp.einsum('enh,ehd->end', h, w2) + b2[:, None, :]
        out = jnp.einsum('end,ne,n->nd', y, sel.astype(x.dtype), tok_w)
        return out.reshape(Bx, Sx, D)

    def _L1_attn_ref(in_seq, theta_K, theta_V, theta_Q, W0, b0):
        import jax, jax.numpy as jnp
        import numpy as np
        B, S, D_IN, D_H = (8, 256, 128, 128)
        LR = 0.01
        'TTT layer: per-token inner SGD step on MSE(W@k+b, v), then predict W@q+b.'
        d_h = W0.shape[0]
        K = jnp.einsum('bsd,ed->bse', in_seq, theta_K)
        V = jnp.einsum('bsd,ed->bse', in_seq, theta_V)
        Q = jnp.einsum('bsd,ed->bse', in_seq, theta_Q)

        def step(carry, kvq):
            W, b = carry
            k, v, q = kvq
            pred = W @ k + b
            g = 2.0 / d_h * (pred - v)
            W = W - LR * jnp.outer(g, k)
            b = b - LR * g
            out = W @ q + b
            return ((W, b), out)

        def run_seq(k_s, v_s, q_s):
            _, ys = jax.lax.scan(step, (W0, b0), (k_s, v_s, q_s))
            return ys
        return jax.vmap(run_seq)(K, V, Q)

    def _L1_ffn_ref(x, Wg, W1, b1, W2, b2):
        import jax, jax.numpy as jnp
        import numpy as np
        B, S, D = (4, 256, 128)
        F = 512
        E = 8
        K = 2
        EPS = 1e-09
        logits = jnp.einsum('bsd,de->bse', x, Wg)
        P = jax.nn.softmax(logits, axis=-1)
        _, topk_idx = jax.lax.top_k(P, K)
        mask = jax.nn.one_hot(topk_idx, E, dtype=x.dtype).sum(-2)
        P_topk = P * mask
        P_norm = P_topk / (P_topk.sum(axis=-1, keepdims=True) + EPS)
        h = jax.nn.gelu(jnp.einsum('bsd,edf->ebsf', x, W1) + b1[:, None, None, :], approximate=False)
        y_e = jnp.einsum('ebsf,efd->ebsd', h, W2) + b2[:, None, None, :]
        y = jnp.einsum('ebsd,bse->bsd', y_e, P_norm)
        return y
    x = L0_attn_x
    xn = _layernorm(x, axis=-1)
    s = _L0_attn_ref(xn, L0_attn_W_qkv, L0_attn_W_out, L0_attn_b_out)
    g = _silu(_L0_ffn_ref(xn, L0_ffn_gate_w, L0_ffn_w1, L0_ffn_b1, L0_ffn_w2, L0_ffn_b2))
    x = x + s * g
    xn = _layernorm(x, axis=-1)
    s = _L1_attn_ref(xn, L1_attn_theta_K, L1_attn_theta_V, L1_attn_theta_Q, L1_attn_W0, L1_attn_b0)
    g = _silu(_L1_ffn_ref(xn, L1_ffn_Wg, L1_ffn_W1, L1_ffn_b1, L1_ffn_W2, L1_ffn_b2))
    x = x + s * g
    return x

_drawn_inputs = setup_inputs


def setup_inputs(seed=0):
    import zlib

    import numpy as np

    out = dict(_drawn_inputs(seed))
    spreads = {'L0_ffn_b1': (0.0, 0.8),
     'L0_ffn_b2': (0.0, 0.8),
     'L1_attn_b0': (0.0, 0.8),
     'L1_ffn_b1': (0.0, 0.8),
     'L1_ffn_b2': (0.0, 0.8)}
    factors = {'L0_attn_W_qkv': 8.0,
     'L0_attn_W_out': 8.0,
     'L0_attn_b_out': 3.683,
     'L0_ffn_gate_w': 3.938,
     'L0_ffn_w1': 3.876,
     'L0_ffn_w2': 3.561,
     'L1_attn_theta_K': 8.0,
     'L1_attn_theta_V': 8.0,
     'L1_attn_theta_Q': 8.0,
     'L1_attn_W0': 8.0,
     'L1_ffn_Wg': 8.0,
     'L1_ffn_W1': 8.0,
     'L1_ffn_W2': 8.0}
    for name, (base, spread) in spreads.items():
        noise = np.random.default_rng([zlib.crc32(name.encode()), seed]).standard_normal(out[name].shape)
        drawn = base * np.exp(spread * noise) if base else spread * noise
        out[name] = jnp.asarray(drawn.astype(out[name].dtype))
    for name, factor in factors.items():
        out[name] = (out[name] * factor).astype(out[name].dtype)
    return out
```

```python
from contextlib import ExitStack

import concourse.bass as bass
from concourse import mybir

F32 = mybir.dt.float32
BF16 = mybir.dt.bfloat16
I32 = mybir.dt.int32
ALU = mybir.AluOpType
ACT = mybir.ActivationFunctionType
AX = mybir.AxisListType

P = 128
LN_EPS = 1e-5
ATT_EPS = 1e-6
NORM_EPS = 1e-9
LR = 0.01
RSQRT_SEED = 0x5F3759DF
EXP_FLOOR = -87.0

TILES = 4
LEVELS = 7
NEWTON = 3
LN_LINKS = 4 + 3 * NEWTON
GATE_LINKS = 15
BLOCK0_LINKS = 2 * LN_LINKS + 2 * GATE_LINKS + 2 + 2 + 2 + 5


def two_block_kernel(nc, x, W_qkv, W_out, b_out, gate_w, w1_0, b1_0, w2_0, b2_0,
                     theta_K, theta_V, theta_Q, W0, b0, Wg, W1, b1, W2, b2, out):
    seqs, seq_len, D = x.shape
    E = gate_w.shape[1]
    HID0 = E * w1_0.shape[2]
    F = W1.shape[2]
    assert D == P and seq_len == 2 * P
    n_tiles = seqs * seq_len // P
    groups = n_tiles // TILES
    J0 = HID0 // P
    JF = F // P
    HT = E * JF
    UNITS = E + 1
    GW = TILES * P
    RATE = 2.0 * LR / D

    x_rows = x.rearrange("s (h p) d -> p (s h) d", p=P)
    out_rows = out.rearrange("s (h p) d -> p (s h) d", p=P)

    ctx = ExitStack()
    with ctx:
        def sb(name, shape, dt=F32):
            return ctx.enter_context(nc.sbuf_tensor(name, shape, dt))

        def bank(name):
            return ctx.enter_context(nc.psum_tensor(name, [P, 512], F32))

        def sem(name):
            return ctx.enter_context(nc.semaphore(name))

        x_all = sb("x_all", [P, n_tiles, D])
        w1_all = sb("w1_all", [P, E, F])
        w2_all = sb("w2_all", [P, HT, D])
        w1_l0 = sb("w1_l0", [P, E, HID0 // E])
        w2_l0 = sb("w2_l0", [P, J0, D])
        b2_l0 = sb("b2_l0", [E, D])
        b2_l1 = sb("b2_l1", [E, D])
        gate0 = sb("gate0", [P, E])
        gate1 = sb("gate1", [P, E])
        nat = sb("nat", [P, 8, P])
        NAT_Q, NAT_K, NAT_V, NAT_OUT, NAT_TK, NAT_TV, NAT_TQ, NAT_W0 = range(8)
        b1_nat = sb("b1_nat", [HT + J0, P])
        rows = sb("rows", [1, 2 * D])
        wqT = sb("wqT", [P, P])
        wkT = sb("wkT", [P, P])
        woutT = sb("woutT", [P, P])
        wvo = sb("wvo", [P, P])
        tkT = sb("tkT", [P, P])
        tqT = sb("tqT", [P, P])
        tvT = sb("tvT", [P, P])
        w0T = sb("w0T", [P, P])
        m_res = sb("m_res", [P, P])
        m_out = sb("m_out", [P, P])
        b1T = sb("b1T", [P, HT + J0])
        bias_rows = sb("bias_rows", [P, 2, D])
        cb0 = sb("cb0", [P, D])

        ident = sb("ident", [P, P])
        ones_row = sb("ones_row", [1, P])
        mask_n = sb("mask_n", [P, P])
        mask_q = sb("mask_q", [P, P])
        mask_x = sb("mask_x", [P, TILES, P])
        mask_lv = sb("mask_lv", [P, LEVELS, P])
        expert_of = sb("expert_of", [E, J0, P], BF16)
        rank_w = sb("rank_w", [P, TILES, E])

        stats = sb("stats", [P, TILES, 6])
        mv = sb("mv", [P, TILES, 2])
        v4 = sb("v4", [P, TILES])
        seed = sb("seed", [P, TILES], I32)
        rstd = sb("rstd", [P, TILES])
        nt_a = sb("nt_a", [P, TILES])
        xn = sb("xn", [P, TILES, D])
        xnT0 = sb("xnT0", [P, GW])
        k0 = sb("k0", [P, TILES, D])
        v0 = sb("v0", [P, TILES, D + 1])
        q0T = sb("q0T", [P, GW])
        kv0 = sb("kv0", [P, TILES // 2, D + 1])
        z0 = sb("z0", [P, TILES])
        s0 = sb("s0", [P, TILES, D])
        d_lg = sb("d_lg", [P, TILES, E])
        th_lg = sb("th_lg", [P, TILES, E])
        num = sb("num", [P, TILES, E])
        den = sb("den", [P, TILES, E])
        ex = sb("ex", [P, TILES, E])
        tie = sb("tie", [P, TILES, E])
        first = sb("first", [P, TILES, E])
        d2 = sb("d2", [P, TILES, E])
        sel = sb("sel", [P, TILES, E])
        r4 = sb("r4", [P, TILES])
        m4 = sb("m4", [P, TILES])
        z4 = sb("z4", [P, TILES])
        tok_w = sb("tok_w", [P, TILES])
        selT = sb("selT", [E, GW])
        selT_b = sb("selT_b", [E, GW], BF16)
        h0T = sb("h0T", [P, J0, GW])
        hg0T = sb("hg0T", [P, J0, GW])
        gg0 = sb("gg0", [P, TILES, D])
        th0 = sb("th0", [P, TILES, D])
        mix = sb("mix", [P, TILES, D])

        xnT1 = [sb(f"xnT1_{i}", [P, GW]) for i in range(2)]
        pw = [sb(f"pw_{i}", [P, TILES, E]) for i in range(2)]
        pT = [sb(f"pT_{i}", [E, GW]) for i in range(2)]

        kT = sb("kT", [P, GW])
        qT = sb("qT", [P, GW])
        nT = sb("nT", [P, TILES, P])
        qkT = sb("qkT", [P, TILES, P])
        crossT = sb("crossT", [P, TILES, P])
        res = sb("res", [P, TILES, D])
        xinv = sb("xinv", [P, TILES, P])
        xinvT = sb("xinvT", [P, TILES, P])
        pn = sb("pn", [P, TILES, P])
        upd = sb("upd", [P, TILES, D])
        res2 = sb("res2", [P, 2, D])
        s1 = sb("s1", [P, TILES, D])

        h1T = sb("h1T", [P, 2, JF, GW])
        y1 = sb("y1", [P, TILES, D])
        th1 = sb("th1", [P, TILES, D])
        mix1 = sb("mix1", [P, TILES, D])

        psH = [bank(f"psH{i}") for i in range(2)]
        psY = [bank(f"psY{i}") for i in range(2)]
        psT = [bank(f"psT{i}") for i in range(2)]
        psC = [bank(f"psC{i}") for i in range(2)]

        def tiles(ps):
            return ps[:, :].rearrange("p (t d) -> p t d", t=TILES)

        x_in = [sem(f"x_in{i}") for i in range(2)]
        w_small = sem("w_small")
        w_l0 = sem("w_l0")
        w_l1 = sem("w_l1")
        consts = sem("consts")
        pool_order = sem("pool_order")
        prep_ps = sem("prep_ps")
        prep_sb = sem("prep_sb")
        prep_dve = sem("prep_dve")
        order0 = sem("order0")
        S = {n: sem(n) for n in (
            "stats0_ready", "stats1_ready", "stats_first", "xn0_ready", "xt0_ps", "xt0_ready", "k0_ps", "k0_ready", "v0_ps", "v0_ready", "q0_ps",
            "q0_ready", "lg0_ps", "lg0_read", "d0_ready", "tanh0_ready", "sel_ready", "kv0_ps",
            "kv0_ready", "att_ps", "s0_ready", "selT_ps", "selT_ready", "selTb_ready",
            "hid0_ps",
            "gelu0_ready",
            "selb_ps",
            "hg0_ready",
            "y0_ps", "gg0_ready", "silu0_ready", "x1_ready", "xn1_ready", "xt1_ps", "xt1_ready",
            "lg1_ps", "lg1_read", "d1_ready", "tanh1_ready", "pw_ready", "pT_ps", "pT_ready",
            "kT_ps", "kT_ready", "qT_ps", "qT_ready", "n_ps", "n_ready", "qk_ps", "qk_ready",
            "cross_ps", "cross_ready", "res_ps", "res_ready",
            "xinv_ready",
            "xinvT_ready",
            "one_ready", *(f"join{lv}_ps" for lv in range(1, LEVELS)),
            "p_ps", "p_ready",
            "xt_ps",
            "u1_ps", "u1_ready", "res2_ps", "res2_ready", "u2_ps", "u2_ready", "o_ps",
            "s1_ready",
            "hid_ps", "gelu_ready",
            "y_ps", "y_added",
            "silu1_ready", "mix1_ready", "x2_ready", "x_out",
        )}

        BLOCK0 = (["ln0", "xt0", "lg0", "k", "v", "q", "kv", "selT", "att"]
                  + [("hid0", j) for j in range(J0)]
                  + ["y0", "mix0", "ln1", "xt1", "lg1", "pT"])
        RECUR = (["kT", "qT", "gram_n", "gram_q", "gram_x", "resid"]
                 + [s for lv in range(1, LEVELS) for s in (("half", lv), ("join", lv))]
                 + ["u1", "cross", "u2", "out"])

        def slots(with_next):
            for n in range(HT):
                rec = RECUR[n * len(RECUR) // HT:(n + 1) * len(RECUR) // HT]
                nxt = BLOCK0[n * len(BLOCK0) // HT:(n + 1) * len(BLOCK0) // HT] if with_next else []
                yield n // JF, n % JF, rec, nxt

        def schedule(eng, first_group, main):
            first_group(0)
            with eng.Fori(0, groups - 2, 2) as g:
                main(g, 0, True)
                main(g + 1, 1, True)
            main(groups - 2, 0, True)
            main(groups - 1, 1, False)

        block = ctx.enter_context(nc.Block())

        @block.sync
        def _(sp):
            half = groups // 2
            sp.dma_start(x_all[:, 0:TILES, :], x_rows[:, 0:TILES, :]).then_inc(x_in[0], 16)
            for n, w in ((NAT_Q, W_qkv[0:D, :]), (NAT_K, W_qkv[D:2 * D, :]),
                         (NAT_V, W_qkv[2 * D:3 * D, :]), (NAT_OUT, W_out),
                         (NAT_TK, theta_K), (NAT_TV, theta_V), (NAT_TQ, theta_Q), (NAT_W0, W0)):
                sp.dma_start(nat[:, n, :], w).then_inc(w_small, 16)
            sp.dma_start(w1_l0[:, :, :], w1_0.rearrange("e d h -> d e h")).then_inc(w_l0, 16)
            sp.dma_start(w2_l0[:, :, :], w2_0.rearrange("e h d -> (e h) d")
                         .rearrange("(j p) d -> p j d", p=P)).then_inc(w_l0, 16)
            sp.dma_start(x_all[:, TILES:, :], x_rows[:, TILES:, :]).then_inc(x_in[1], 16)
            sp.dma_start(w1_all[:, :, :], W1.rearrange("e d f -> d e f")).then_inc(w_l1, 16)
            sp.dma_start(w2_all[:, :, :], W2.rearrange("e f d -> (e f) d")
                         .rearrange("(k p) d -> p k d", p=P)).then_inc(w_l1, 16)

            def store(g):
                sp.wait_ge(S["x2_ready"], g + 1)
                sp.dma_start(out_rows[:, bass.ds(g * TILES, TILES), :],
                             x_all[:, bass.ds(g * TILES, TILES), :]).then_inc(S["x_out"], 16)

            with sp.Fori(0, groups) as g:
                store(g)
            sp.wait_ge(S["x_out"], 16 * groups)

        @block.gpsimd
        def _(pool):
            steps = [0]

            def ordered(ins):
                ins.then_inc(pool_order, 1)
                steps[0] += 1
                pool.wait_ge(pool_order, steps[0])

            ordered(pool.memset(ident[:, :], 0.0))
            pool.affine_select(out=ident[:, :], in_=ident[:, :], compare_op=ALU.not_equal, fill=1.0,
                               base=0, pattern=[[-1, P]], channel_multiplier=1).then_inc(consts, 1)
            pool.memset(ones_row[:, :], 1.0)
            pool.memset(v0[:, :, D:D + 1], 1.0)
            for e in range(E):
                pool.memset(rank_w[:, :, e:e + 1], float(E - e))
            pool.memset(mask_x[:, 0::2, :], -RATE)
            pool.memset(mask_x[:, 1::2, :], 1.0)
            pool.memset(mask_n[:, :], -RATE)
            pool.memset(mask_q[:, :], 1.0)
            pool.memset(mask_lv[:, :, :], 0.0)
            ordered(pool.memset(expert_of[:, :, :], 0.0))
            pool.affine_select(out=mask_n[:, :], in_=mask_n[:, :], compare_op=ALU.is_gt, fill=0.0,
                               base=0, pattern=[[1, P]], channel_multiplier=-1)
            pool.affine_select(out=mask_q[:, :], in_=mask_q[:, :], compare_op=ALU.is_ge, fill=0.0,
                               base=0, pattern=[[1, P]], channel_multiplier=-1)
            eo = expert_of[:, :, :].rearrange("e j (a h) -> e (j a) h", h=HID0 // E)
            pool.affine_select(out=eo, in_=eo, compare_op=ALU.not_equal, fill=1.0,
                               base=0, pattern=[[-1, E], [0, HID0 // E]], channel_multiplier=1)
            for lv in range(LEVELS):
                b = 1 << lv
                odd = mask_lv[:, lv, :].rearrange("p (n a b) -> p n a b", a=2, b=b)[:, :, 1, :]
                ordered(pool.memset(odd, 1.0))
                ordered(pool.affine_select(out=odd, in_=odd, compare_op=ALU.is_ge, fill=0.0, base=0,
                                           pattern=[[-2 * b, P // (2 * b)], [0, b]],
                                           channel_multiplier=1))
                last = pool.affine_select(out=odd, in_=odd, compare_op=ALU.is_ge, fill=0.0,
                                          base=b - 1, pattern=[[2 * b, P // (2 * b)], [0, b]],
                                          channel_multiplier=-1)
            last.then_inc(consts, 1)

        def load_small(act):
            act.dma_start(b1_nat[0:HT, :], b1.rearrange("e (j p) -> (e j) p", p=P)).then_inc(w_small, 16)
            act.dma_start(b1_nat[HT:HT + J0, :], b1_0.rearrange("e h -> (e h)")
                          .rearrange("(j p) -> j p", p=P)).then_inc(w_small, 16)
            act.dma_start(rows[:, 0:D], b_out.rearrange("(a n) -> a n", a=1)).then_inc(w_small, 16)
            act.dma_start(rows[:, D:2 * D], b0.rearrange("(a n) -> a n", a=1)).then_inc(w_small, 16)
            act.dma_start(gate0[:, :], gate_w).then_inc(w_small, 16)
            act.dma_start(gate1[:, :], Wg).then_inc(w_small, 16)
            act.dma_start(b2_l0[:, :], b2_0).then_inc(w_small, 16)
            act.dma_start(b2_l1[:, :], b2).then_inc(w_small, 16)

        SMALL_LOADS = 8 + 8

        @block.tensor
        def _(pe):
            mm = nc.tensor.matmul
            tr = nc.tensor.transpose

            pe.wait_ge(consts, 2)
            pe.wait_ge(w_small, 16 * SMALL_LOADS)
            for n, i in enumerate((NAT_Q, NAT_K, NAT_OUT, NAT_TK)):
                last = tr(psC[0][:, n * P:(n + 1) * P], nat[:, i, :], ident[:, :])
            last.then_inc(prep_ps, 1)
            for n, i in enumerate((NAT_TQ, NAT_TV, NAT_W0)):
                tr(psC[1][:, n * P:(n + 1) * P], nat[:, i, :], ident[:, :])
            tr(psC[1][:, 3 * P:3 * P + HT + J0], b1_nat[:, :],
               ident[0:HT + J0, 0:HT + J0]).then_inc(prep_ps, 1)
            mm(psT[0][:, 0:2 * D], ones_row[:, :], rows[:, :], start=True, stop=True).then_inc(prep_ps, 1)
            pe.wait_ge(prep_sb, 2)
            mm(psT[1][:, 0:P], nat[:, NAT_V, :], woutT[:, :], start=True, stop=True)
            mm(psT[1][:, P:2 * P], nat[:, NAT_TK, :], w0T[:, :], start=True, stop=True)
            mm(psT[1][:, 2 * P:3 * P], nat[:, NAT_TQ, :], w0T[:, :], start=True, stop=True).then_inc(prep_ps, 1)
            pe.wait_ge(prep_sb, 5)
            pe.wait_ge(w_l0, 32)

            def block0(step, h, par):
                def ready(name, per=1, k=1):
                    pe.wait_ge(S[name], h * per + k)

                if step == "xt0":
                    ready("xn0_ready")
                    for t in range(TILES):
                        last = tr(psC[0][:, t * P:(t + 1) * P], xn[:, t, :], ident[:, :])
                    last.then_inc(S["xt0_ps"], 1)
                elif step == "lg0":
                    ready("xt0_ready")
                    for t in range(TILES):
                        last = mm(psC[1][:, t * E:(t + 1) * E], xnT0[:, t * P:(t + 1) * P], gate0[:, :],
                                  start=True, stop=True)
                    last.then_inc(S["lg0_ps"], 1)
                elif step == "k":
                    for t in range(TILES):
                        last = mm(psC[0][:, t * P:(t + 1) * P], xnT0[:, t * P:(t + 1) * P], wkT[:, :],
                                  start=True, stop=True)
                    last.then_inc(S["k0_ps"], 1)
                elif step == "v":
                    ready("lg0_read")
                    for t in range(TILES):
                        last = mm(psC[1][:, t * P:(t + 1) * P], xnT0[:, t * P:(t + 1) * P], wvo[:, :],
                                  start=True, stop=True)
                    last.then_inc(S["v0_ps"], 1)
                elif step == "q":
                    ready("k0_ready")
                    mm(psC[0][:, :], wqT[:, :], xnT0[:, :], start=True, stop=True).then_inc(S["q0_ps"], 1)
                elif step == "kv":
                    ready("v0_ready")
                    for s in range(2):
                        for t in range(2):
                            last = mm(psC[1][:, s * 256:s * 256 + D + 1], k0[:, 2 * s + t, :],
                                      v0[:, 2 * s + t, :], start=(t == 0), stop=(t == 1))
                    last.then_inc(S["kv0_ps"], 1)
                elif step == "selT":
                    ready("q0_ready")
                    ready("sel_ready")
                    for t in range(TILES):
                        last = tr(psC[0][0:E, t * P:(t + 1) * P], sel[:, t, :], ident[:, :])
                    last.then_inc(S["selT_ps"], 1)
                elif step == "att":
                    ready("kv0_ready")
                    ready("selT_ready")
                    for t in range(TILES):
                        qt = q0T[:, t * P:(t + 1) * P]
                        mm(psC[0][:, t * P:(t + 1) * P], qt, kv0[:, t // 2, 0:D], start=True, stop=True)
                        last = mm(psC[1][:, t:t + 1], qt, kv0[:, t // 2, D:D + 1], start=True, stop=True)
                    last.then_inc(S["att_ps"], 1)
                elif step[0] == "hid0":
                    j = step[1]
                    if j == 0:
                        ready("s0_ready")
                        ready("selTb_ready")
                    else:
                        ready("hg0_ready", J0, j)
                    w = w1_l0[:, :, :].rearrange("d e h -> d (e h)")[:, j * P:(j + 1) * P]
                    mm(psC[0][:, :], w, xnT0[:, :], start=True, stop=True).then_inc(S["hid0_ps"], 1)
                    mm(psC[1][:, :], expert_of[:, j, :], selT_b[:, :], start=True,
                       stop=True).then_inc(S["selb_ps"], 1)
                elif step == "y0":
                    ready("hg0_ready", J0, J0)
                    for t in range(TILES):
                        o = psC[0][:, t * P:(t + 1) * P]
                        for j in range(J0):
                            mm(o, hg0T[:, j, t * P:(t + 1) * P], w2_l0[:, j, :], start=(j == 0), stop=False)
                        last = mm(o, selT[:, t * P:(t + 1) * P], b2_l0[:, :], start=False, stop=True)
                    last.then_inc(S["y0_ps"], 1)
                elif step == "xt1":
                    ready("xn1_ready")
                    for t in range(TILES):
                        last = tr(psC[1][:, t * P:(t + 1) * P], xn[:, t, :], ident[:, :])
                    last.then_inc(S["xt1_ps"], 1)
                elif step == "lg1":
                    ready("gg0_ready")
                    ready("xt1_ready")
                    for t in range(TILES):
                        last = mm(psC[0][:, t * E:(t + 1) * E], xnT1[par][:, t * P:(t + 1) * P],
                                  gate1[:, :], start=True, stop=True)
                    last.then_inc(S["lg1_ps"], 1)
                elif step == "pT":
                    ready("pw_ready")
                    for t in range(TILES):
                        last = tr(psC[1][0:E, t * P:(t + 1) * P], pw[par][:, t, :], ident[:, :])
                    last.then_inc(S["pT_ps"], 1)

            def recur(step, g, par):
                def ready(name, per=1, k=1):
                    pe.wait_ge(S[name], g * per + k)

                xT = xnT1[par]

                def col(t):
                    return slice(t * P, (t + 1) * P)

                if step == "kT":
                    mm(psT[0][:, :], tkT[:, :], xT[:, :], start=True, stop=True).then_inc(S["kT_ps"], 1)
                elif step == "qT":
                    pe.wait_ge(S["s1_ready"], g + 1)
                    mm(psT[1][:, :], tqT[:, :], xT[:, :], start=True, stop=True).then_inc(S["qT_ps"], 1)
                elif step == "gram_n":
                    ready("kT_ready")
                    for t in range(TILES):
                        last = mm(psT[0][:, col(t)], kT[:, col(t)], kT[:, col(t)], start=True, stop=True)
                    last.then_inc(S["n_ps"], 1)
                elif step == "gram_q":
                    ready("qT_ready")
                    for t in range(TILES):
                        last = mm(psT[1][:, col(t)], kT[:, col(t)], qT[:, col(t)], start=True, stop=True)
                    last.then_inc(S["qk_ps"], 1)
                elif step == "gram_x":
                    ready("n_ready")
                    for s in range(2):
                        a, b = col(2 * s), col(2 * s + 1)
                        mm(psT[0][:, a], kT[:, a], kT[:, b], start=True, stop=True)
                        last = mm(psT[0][:, b], kT[:, a], qT[:, b], start=True, stop=True)
                    last.then_inc(S["cross_ps"], 1)
                elif step == "resid":
                    ready("qk_ready")
                    for t in range(TILES):
                        last = mm(psT[1][:, col(t)], xT[:, col(t)], m_res[:, :], start=True, stop=True)
                    last.then_inc(S["res_ps"], 1)
                elif step[0] == "half":
                    lv = step[1]
                    if lv == 1:
                        ready("cross_ready")
                    ready("xinv_ready", LEVELS - 1, lv)
                    for t in range(TILES):
                        last = mm(psT[0][:, col(t)], nT[:, t, :], xinv[:, t, :], start=True, stop=True)
                    last.then_inc(S["p_ps"], 1)
                elif step[0] == "join":
                    lv = step[1]
                    if lv == 1:
                        ready("res_ready")
                    ready("xinvT_ready", LEVELS, lv)
                    ready("p_ready", LEVELS - 1, lv)
                    for t in range(TILES):
                        last = mm(psT[1][:, col(t)], pn[:, t, :], xinvT[:, t, :], start=True, stop=True)
                    last.then_inc(S[f"join{lv}_ps"], 1)
                    if lv == LEVELS - 2:
                        ready("xinvT_ready", LEVELS, LEVELS - 1)
                        for t in range(TILES):
                            last = tr(psT[0][:, col(t)], xinvT[:, t, :], ident[:, :])
                        last.then_inc(S["xt_ps"], 1)
                elif step == "u1":
                    ready("xinvT_ready", LEVELS, LEVELS)
                    for t in (0, 2):
                        last = mm(psT[0][:, col(t)], xinvT[:, t, :], res[:, t, :], start=True, stop=True)
                    last.then_inc(S["u1_ps"], 1)
                elif step == "cross":
                    ready("u1_ready")
                    for s in range(2):
                        last = mm(psT[1][:, col(s)], crossT[:, 2 * s, :], upd[:, 2 * s, :],
                                  start=True, stop=True)
                    last.then_inc(S["res2_ps"], 1)
                elif step == "u2":
                    ready("res2_ready")
                    for s in range(2):
                        last = mm(psT[0][:, col(s)], xinvT[:, 2 * s + 1, :], res2[:, s, :],
                                  start=True, stop=True)
                    last.then_inc(S["u2_ps"], 1)
                elif step == "out":
                    ready("u2_ready")
                    for t in range(TILES):
                        o = psT[1][:, col(t)]
                        mm(o, xT[:, col(t)], m_out[:, :], start=True, stop=False)
                        if t % 2:
                            mm(o, crossT[:, t, :], upd[:, t - 1, :], start=False, stop=False)
                        last = mm(o, qkT[:, t, :], upd[:, t, :], start=False, stop=True)
                    last.then_inc(S["o_ps"], 1)

            def expert_in(g, par, e, j):
                n = e * JF + j
                if n >= 2:
                    pe.wait_ge(S["gelu_ready"], g * HT + n - 1)
                mm(psH[n % 2][:, :], w1_all[:, e, j * P:(j + 1) * P], xnT1[par][:, :],
                   start=True, stop=True).then_inc(S["hid_ps"], 1)

            def expert_out(g, e, t):
                if t == 0:
                    pe.wait_ge(S["gelu_ready"], g * HT + (e + 1) * JF)
                    if e >= 1:
                        pe.wait_ge(S["y_added"], g * UNITS + e + 1)
                for k in range(JF):
                    last = mm(psY[e % 2][:, t * P:(t + 1) * P], h1T[:, e % 2, k, t * P:(t + 1) * P],
                              w2_all[:, e * JF + k, :], start=(k == 0), stop=(k == JF - 1))
                if t == TILES - 1:
                    last.then_inc(S["y_ps"], 1)

            def main(g, par, with_next):
                pe.wait_ge(S["pT_ready"], g + 1)
                pe.wait_ge(S["y_added"], g * UNITS + 1)
                for t in range(TILES):
                    last = mm(psY[1][:, t * P:(t + 1) * P], pT[par][:, t * P:(t + 1) * P], b2_l1[:, :],
                              start=True, stop=True)
                last.then_inc(S["y_ps"], 1)
                for e, j, rec, nxt in slots(with_next):
                    expert_in(g, par, e, j)
                    for s in rec:
                        recur(s, g, par)
                    if e:
                        expert_out(g, e - 1, j)
                    for s in nxt:
                        block0(s, g + 1, 1 - par)
                for t in range(TILES):
                    expert_out(g, E - 1, t)

            def first_group(h):
                for s in BLOCK0:
                    block0(s, h, 0)
                pe.wait_ge(w_l1, 32)

            schedule(pe, first_group, main)

        @block.scalar
        def _(act):
            load_small(act)
            f = nc.scalar.activation
            act.wait_ge(prep_ps, 1)
            for n, w in enumerate((wqT, wkT, woutT, tkT)):
                last = f(w[:, :], psC[0][:, n * P:(n + 1) * P], ACT.Copy)
            last.then_inc(prep_sb, 1)
            act.wait_ge(prep_ps, 2)
            for n, w in enumerate((tqT, tvT, w0T)):
                f(w[:, :], psC[1][:, n * P:(n + 1) * P], ACT.Copy)
            f(b1T[:, :], psC[1][:, 3 * P:3 * P + HT + J0], ACT.Copy).then_inc(prep_sb, 1)
            act.wait_ge(prep_ps, 3)
            f(bias_rows[:, :, :], psT[0][:, 0:2 * D].rearrange("p (a d) -> p a d", a=2),
              ACT.Copy).then_inc(prep_sb, 1)
            act.wait_ge(prep_sb, 3)
            f(cb0[:, :], bias_rows[:, 1, :], ACT.Copy, scale=RATE).then_inc(prep_sb, 1)
            act.wait_ge(prep_ps, 4)
            f(wvo[:, :], psT[1][:, 0:P], ACT.Copy)
            f(m_out[:, :], psT[1][:, 2 * P:3 * P], ACT.Copy).then_inc(prep_dve, 1)

            def block0(step, h, par):
                def ready(name, per=1, k=1):
                    act.wait_ge(S[name], h * per + k)

                if step == "xt0":
                    ready("xt0_ps")
                    f(xnT0[:, :], psC[0][:, :], ACT.Copy).then_inc(S["xt0_ready"], 1)
                elif step == "v":
                    ready("v0_ps")
                    f(v0[:, :, 0:D], tiles(psC[1]), ACT.Copy).then_inc(S["v0_ready"], 1)
                elif step == "kv":
                    ready("kv0_ps")
                    f(kv0[:, :, :], psC[1][:, :].rearrange("p (s d) -> p s d", s=2)[:, :, 0:D + 1],
                      ACT.Copy).then_inc(S["kv0_ready"], 1)
                elif step == "lg0":
                    ready("d0_ready")
                    f(th_lg[:, :, :], d_lg[:, :, :], ACT.Tanh, scale=0.5).then_inc(S["tanh0_ready"], 1)
                elif step == "selT":
                    ready("selT_ready")
                    f(selT_b[:, :], selT[:, :], ACT.Copy).then_inc(S["selTb_ready"], 1)
                elif step[0] == "hid0":
                    j = step[1]
                    ready("hid0_ps", J0, j + 1)
                    f(h0T[:, j, :], psC[0][:, :], ACT.Gelu,
                      bias=b1T[:, HT + j:HT + j + 1]).then_inc(S["gelu0_ready"], 1)
                elif step == "mix0":
                    ready("gg0_ready")
                    f(th0[:, :, :], gg0[:, :, :], ACT.Tanh, scale=0.5).then_inc(S["silu0_ready"], 1)
                elif step == "xt1":
                    ready("xt1_ps")
                    f(xnT1[par][:, :], psC[1][:, :], ACT.Copy).then_inc(S["xt1_ready"], 1)
                elif step == "lg1":
                    ready("d1_ready")
                    f(th_lg[:, :, :], d_lg[:, :, :], ACT.Tanh, scale=0.5).then_inc(S["tanh1_ready"], 1)
                elif step == "pT":
                    ready("pT_ps")
                    f(pT[par][:, :], psC[1][0:E, :], ACT.Copy).then_inc(S["pT_ready"], 1)

            def recur(step, g, par):
                def ready(name, per=1, k=1):
                    act.wait_ge(S[name], g * per + k)

                if step == "kT":
                    ready("kT_ps")
                    f(kT[:, :], psT[0][:, :], ACT.Copy).then_inc(S["kT_ready"], 1)
                elif step == "qT":
                    ready("qT_ps")
                    f(qT[:, :], psT[1][:, :], ACT.Copy).then_inc(S["qT_ready"], 1)
                elif step[0] == "half":
                    lv = step[1]
                    ready("p_ps", LEVELS - 1, lv)
                    f(pn[:, :, :], tiles(psT[0]), ACT.Copy).then_inc(S["p_ready"], 1)
                elif step[0] == "join" and step[1] == LEVELS - 2:
                    ready("xt_ps")
                    f(xinv[:, :, :], tiles(psT[0]), ACT.Copy).then_inc(S["xinv_ready"], 1)
                elif step == "u1":
                    ready("u1_ps")
                    f(upd[:, 0::2, :], tiles(psT[0])[:, 0::2, :], ACT.Copy).then_inc(S["u1_ready"], 1)
                elif step == "u2":
                    ready("u2_ps")
                    f(upd[:, 1::2, :], tiles(psT[0])[:, 0:2, :], ACT.Copy).then_inc(S["u2_ready"], 1)

            def main(g, par, with_next):
                for e, j, rec, nxt in slots(with_next):
                    n = e * JF + j
                    if j == 0 and e >= 2:
                        act.wait_ge(S["y_ps"], g * UNITS + e)
                    act.wait_ge(S["hid_ps"], g * HT + n + 1)
                    f(h1T[:, e % 2, j, :], psH[n % 2][:, :], ACT.Gelu,
                      bias=b1T[:, n:n + 1]).then_inc(S["gelu_ready"], 1)
                    for s in rec:
                        recur(s, g, par)
                    for s in nxt:
                        block0(s, g + 1, 1 - par)
                act.wait_ge(S["y_added"], (g + 1) * UNITS + 1)
                f(th1[:, :, :], y1[:, :, :], ACT.Tanh, scale=0.5).then_inc(S["silu1_ready"], 1)

            def first_group(h):
                for s in BLOCK0:
                    block0(s, h, 0)

            schedule(act, first_group, main)

        @block.vector
        def _(dve):
            v = nc.vector
            links = [0]

            def wait_apart(value, *signals):
                dve.wait_ge(consts, 2)
                for s in signals:
                    dve.wait_ge(S[s], value)

            dve.wait_ge(prep_dve, 1)
            v.tensor_tensor(m_res[:, :], tvT[:, :], psT[1][:, P:2 * P], ALU.subtract).then_inc(prep_dve, 1)
            dve.wait_ge(prep_dve, 2)
            v.tensor_scalar(m_res[:, :], m_res[:, :], RATE, None, ALU.mult).then_inc(prep_sb, 1)
            dve.wait_ge(consts, 2)
            dve.sem_inc(S["s1_ready"], 1)
            dve.sem_inc(S["y_added"], 1)

            def bc(ap):
                return ap.unsqueeze(2).broadcast_to([P, TILES, E])

            def layer_norm(h, link, stats_ready, done):
                counted = not isinstance(h, int) or h > 0
                for t in range(TILES):
                    last = v.bn_stats(stats[:, t, :], x_all[:, bass.ds(h * TILES + t, 1), :])
                last.then_inc(S[stats_ready] if counted else S["stats_first"], 1)
                if counted:
                    wait_apart(h, stats_ready)
                else:
                    dve.wait_ge(S["stats_first"], 1 if stats_ready == "stats0_ready" else 2)
                for t in range(TILES):
                    last = v.bn_aggr(mv[:, t, :], stats[:, t, :])
                link(last)
                link(v.tensor_scalar(v4[:, :], mv[:, :, 1], LN_EPS, None, ALU.add))
                link(v.tensor_scalar(seed[:, :], v4[:, :].bitcast(I32), 1, None, ALU.logical_shift_right))
                link(v.tensor_scalar(rstd[:, :].bitcast(I32), seed[:, :], -1.0, float(RSQRT_SEED),
                                     ALU.mult, ALU.add))
                for _ in range(NEWTON):
                    link(v.scalar_tensor_tensor(nt_a[:, :], rstd[:, :], -0.5, rstd[:, :],
                                                ALU.mult, ALU.mult))
                    link(v.tensor_tensor(nt_a[:, :], nt_a[:, :], v4[:, :], ALU.mult))
                    link(v.scalar_tensor_tensor(rstd[:, :], nt_a[:, :], 1.5, rstd[:, :],
                                                ALU.add, ALU.mult))
                for t in range(TILES):
                    last = v.tensor_scalar(xn[:, t:t + 1, :], x_all[:, bass.ds(h * TILES + t, 1), :],
                                           mv[:, t, 0:1], rstd[:, t:t + 1], ALU.subtract, ALU.mult)
                last.then_inc(done, 1)

            def gate(ps, link, h, read, d_ready, tanh_ready):
                lg = ps[:, 0:TILES * E].rearrange("p (t e) -> p t e", e=E)
                link(v.tensor_reduce(m4[:, :], lg, AX.X, ALU.max))
                last = v.tensor_tensor(d_lg[:, :, :], lg, bc(m4[:, :]), ALU.subtract)
                last.then_inc(read, 1)
                dve.wait_ge(read, h + 1)
                v.tensor_scalar(d_lg[:, :, :], d_lg[:, :, :], EXP_FLOOR, None, ALU.max).then_inc(d_ready, 1)
                dve.wait_ge(d_ready, h + 1)
                link(v.scalar_tensor_tensor(tie[:, :, :], d_lg[:, :, :], 0.0, rank_w[:, :, :],
                                            ALU.is_equal, ALU.mult))
                link(v.tensor_reduce(r4[:, :], tie[:, :, :], AX.X, ALU.max))
                link(v.tensor_tensor(first[:, :, :], tie[:, :, :], bc(r4[:, :]), ALU.is_equal))
                link(v.scalar_tensor_tensor(d2[:, :, :], first[:, :, :], -1e30, d_lg[:, :, :],
                                            ALU.mult, ALU.add))
                link(v.tensor_reduce(m4[:, :], d2[:, :, :], AX.X, ALU.max))
                link(v.tensor_tensor(tie[:, :, :], d2[:, :, :], bc(m4[:, :]), ALU.is_equal))
                link(v.tensor_tensor(tie[:, :, :], tie[:, :, :], rank_w[:, :, :], ALU.mult))
                link(v.tensor_reduce(r4[:, :], tie[:, :, :], AX.X, ALU.max))
                link(v.tensor_tensor(tie[:, :, :], tie[:, :, :], bc(r4[:, :]), ALU.is_equal))
                v.tensor_tensor(sel[:, :, :], first[:, :, :], tie[:, :, :], ALU.add)
                dve.wait_ge(tanh_ready, h + 1)
                v.tensor_scalar(num[:, :, :], th_lg[:, :, :], 1.0, None, ALU.add)
                link(v.tensor_scalar(den[:, :, :], th_lg[:, :, :], -1.0, 1.0, ALU.mult, ALU.add))
                link(v.reciprocal(den[:, :, :], den[:, :, :]))
                link(v.tensor_tensor(ex[:, :, :], num[:, :, :], den[:, :, :], ALU.mult))
                link(v.tensor_reduce(z4[:, :], ex[:, :, :], AX.X, ALU.add))
                link(v.reciprocal(z4[:, :], z4[:, :]))

            def block0(step, h, par):
                def ready(name, per=1, k=1):
                    dve.wait_ge(S[name], h * per + k)

                def link(ins):
                    ins.then_inc(order0, 1)
                    links[0] += 1
                    dve.wait_ge(order0, h * BLOCK0_LINKS + links[0])

                if step == "ln0":
                    links[0] = 0
                    layer_norm(h, link, "stats0_ready", S["xn0_ready"])
                elif step == "lg0":
                    ready("lg0_ps")
                    gate(psC[1], link, h, S["lg0_read"], S["d0_ready"], S["tanh0_ready"])
                    link(v.tensor_tensor(ex[:, :, :], ex[:, :, :], sel[:, :, :], ALU.mult))
                    link(v.tensor_reduce(m4[:, :], ex[:, :, :], AX.X, ALU.add))
                    v.tensor_tensor(tok_w[:, :], m4[:, :], z4[:, :], ALU.mult).then_inc(S["sel_ready"], 1)
                elif step == "k":
                    ready("k0_ps")
                    v.tensor_scalar(k0[:, :, :], tiles(psC[0]), 0.0, ATT_EPS, ALU.max,
                                    ALU.add).then_inc(S["k0_ready"], 1)
                elif step == "q":
                    ready("q0_ps")
                    v.tensor_scalar(q0T[:, :], psC[0][:, :], 0.0, ATT_EPS, ALU.max,
                                    ALU.add).then_inc(S["q0_ready"], 1)
                elif step == "selT":
                    ready("selT_ps")
                    v.tensor_copy(selT[:, :], psC[0][0:E, :]).then_inc(S["selT_ready"], 1)
                elif step == "att":
                    ready("att_ps")
                    link(v.tensor_scalar(z0[:, :], psC[1][:, 0:TILES], ATT_EPS, None, ALU.add))
                    link(v.reciprocal(z0[:, :], z0[:, :]))
                    for t in range(TILES):
                        last = v.scalar_tensor_tensor(s0[:, t, :], psC[0][:, t * P:(t + 1) * P],
                                                      z0[:, t:t + 1], bias_rows[:, 0, :],
                                                      ALU.mult, ALU.add)
                    last.then_inc(S["s0_ready"], 1)
                elif step[0] == "hid0":
                    j = step[1]
                    ready("gelu0_ready", J0, j + 1)
                    ready("selb_ps", J0, j + 1)
                    v.tensor_tensor(hg0T[:, j, :], h0T[:, j, :], psC[1][:, :],
                                    ALU.mult).then_inc(S["hg0_ready"], 1)
                elif step == "y0":
                    ready("y0_ps")
                    v.tensor_tensor(gg0[:, :, :], tiles(psC[0]),
                                    tok_w[:, :].unsqueeze(2).broadcast_to([P, TILES, D]),
                                    ALU.mult).then_inc(S["gg0_ready"], 1)
                elif step == "mix0":
                    ready("gg0_ready")
                    link(v.tensor_tensor(mix[:, :, :], s0[:, :, :], gg0[:, :, :], ALU.mult))
                    ready("silu0_ready")
                    link(v.scalar_tensor_tensor(mix[:, :, :], th0[:, :, :], 1.0, mix[:, :, :],
                                                ALU.add, ALU.mult))
                    xg = x_all[:, bass.ds(h * TILES, TILES), :]
                    v.scalar_tensor_tensor(xg, mix[:, :, :], 0.5, xg, ALU.mult,
                                           ALU.add).then_inc(S["x1_ready"], 1)
                elif step == "ln1":
                    wait_apart(h + 1, "x1_ready")
                    layer_norm(h, link, "stats1_ready", S["xn1_ready"])
                elif step == "lg1":
                    ready("lg1_ps")
                    gate(psC[0], link, h, S["lg1_read"], S["d1_ready"], S["tanh1_ready"])
                    w = pw[par][:, :, :]
                    link(v.tensor_tensor(ex[:, :, :], ex[:, :, :], bc(z4[:, :]), ALU.mult))
                    link(v.tensor_tensor(ex[:, :, :], ex[:, :, :], sel[:, :, :], ALU.mult))
                    link(v.tensor_reduce(m4[:, :], ex[:, :, :], AX.X, ALU.add))
                    link(v.tensor_scalar(m4[:, :], m4[:, :], NORM_EPS, None, ALU.add))
                    link(v.reciprocal(m4[:, :], m4[:, :]))
                    v.tensor_tensor(w, ex[:, :, :], bc(m4[:, :]), ALU.mult).then_inc(S["pw_ready"], 1)
                elif step == "pT":
                    assert links[0] == BLOCK0_LINKS

            def recur(step, g, par):
                def ready(name, per=1, k=1):
                    dve.wait_ge(S[name], g * per + k)

                def four(m):
                    return m.unsqueeze(1).broadcast_to([P, TILES, P])

                if step == "gram_n":
                    ready("n_ps")
                    v.scalar_tensor_tensor(nT[:, :, :], tiles(psT[0]), 1.0, four(mask_n[:, :]),
                                           ALU.add, ALU.mult).then_inc(S["n_ready"], 1)
                elif step == "gram_q":
                    ready("qk_ps")
                    v.scalar_tensor_tensor(qkT[:, :, :], tiles(psT[1]), 1.0, four(mask_q[:, :]),
                                           ALU.add, ALU.mult).then_inc(S["qk_ready"], 1)
                    v.tensor_copy(xinvT[:, :, :], four(ident[:, :])).then_inc(S["one_ready"], 1)
                    wait_apart(g + 1, "one_ready", "n_ready")
                    v.copy_predicated(xinvT[:, :, :], four(mask_lv[:, 0, :].bitcast(I32)),
                                      nT[:, :, :]).then_inc(S["xinvT_ready"], 1)
                    ready("xinvT_ready", LEVELS, 1)
                    v.transpose(xinv[:, :, :], xinvT[:, :, :]).then_inc(S["xinv_ready"], 1)
                elif step == "gram_x":
                    ready("cross_ps")
                    v.scalar_tensor_tensor(crossT[:, :, :], tiles(psT[0]), 1.0, mask_x[:, :, :],
                                           ALU.add, ALU.mult).then_inc(S["cross_ready"], 1)
                elif step == "resid":
                    ready("res_ps")
                    v.tensor_tensor(res[:, :, :], tiles(psT[1]), four(cb0[:, :]),
                                    ALU.subtract).then_inc(S["res_ready"], 1)
                elif step[0] == "join":
                    lv = step[1]
                    wait_apart(g + 1, f"join{lv}_ps")
                    v.copy_predicated(xinvT[:, :, :], four(mask_lv[:, lv, :].bitcast(I32)),
                                      tiles(psT[1])).then_inc(S["xinvT_ready"], 1)
                    if lv < LEVELS - 2:
                        ready("xinvT_ready", LEVELS, lv + 1)
                        v.transpose(xinv[:, :, :], xinvT[:, :, :]).then_inc(S["xinv_ready"], 1)
                elif step == "cross":
                    ready("res2_ps")
                    v.tensor_tensor(res2[:, :, :], tiles(psT[1])[:, 0:2, :], res[:, 1::2, :],
                                    ALU.add).then_inc(S["res2_ready"], 1)
                elif step == "out":
                    ready("o_ps")
                    v.tensor_tensor(s1[:, :, :], tiles(psT[1]), four(bias_rows[:, 1, :]),
                                    ALU.add).then_inc(S["s1_ready"], 1)

            def add_unit(g, par, m):
                dve.wait_ge(S["y_ps"], g * UNITS + m + 1)
                if m == 0:
                    v.tensor_copy(y1[:, :, :], tiles(psY[1])).then_inc(S["y_added"], 1)
                    return
                e = m - 1
                dve.wait_ge(S["y_added"], g * UNITS + m + 1)
                for t in range(TILES):
                    last = v.scalar_tensor_tensor(y1[:, t, :], psY[e % 2][:, t * P:(t + 1) * P],
                                                  pw[par][:, t, e:e + 1], y1[:, t, :],
                                                  ALU.mult, ALU.add)
                last.then_inc(S["y_added"], 1)

            def main(g, par, with_next):
                add_unit(g, par, 0)
                for e, j, rec, nxt in slots(with_next):
                    for s in rec:
                        recur(s, g, par)
                    if e and j == JF - 1:
                        add_unit(g, par, e)
                    for s in nxt:
                        block0(s, g + 1, 1 - par)
                add_unit(g, par, E)
                dve.wait_ge(S["y_added"], (g + 1) * UNITS + 1)
                dve.wait_ge(S["s1_ready"], g + 2)
                v.tensor_tensor(mix1[:, :, :], s1[:, :, :], y1[:, :, :],
                                ALU.mult).then_inc(S["mix1_ready"], 1)
                dve.wait_ge(S["mix1_ready"], 2 * g + 1)
                dve.wait_ge(S["silu1_ready"], g + 1)
                v.scalar_tensor_tensor(mix1[:, :, :], th1[:, :, :], 1.0, mix1[:, :, :],
                                       ALU.add, ALU.mult).then_inc(S["mix1_ready"], 1)
                dve.wait_ge(S["mix1_ready"], 2 * g + 2)
                xg = x_all[:, bass.ds(g * TILES, TILES), :]
                v.scalar_tensor_tensor(xg, mix1[:, :, :], 0.5, xg, ALU.mult,
                                       ALU.add).then_inc(S["x2_ready"], 1)

            def first_group(h):
                dve.wait_ge(x_in[0], 16)
                for s in BLOCK0:
                    block0(s, h, 0)
                dve.wait_ge(x_in[1], 16)

            schedule(dve, first_group, main)


_INS = ['L0_attn_x', 'L0_attn_W_qkv', 'L0_attn_W_out', 'L0_attn_b_out', 'L0_ffn_gate_w', 'L0_ffn_w1',
        'L0_ffn_b1', 'L0_ffn_w2', 'L0_ffn_b2', 'L1_attn_theta_K', 'L1_attn_theta_V',
        'L1_attn_theta_Q', 'L1_attn_W0', 'L1_attn_b0', 'L1_ffn_Wg', 'L1_ffn_W1', 'L1_ffn_b1',
        'L1_ffn_W2', 'L1_ffn_b2']
_OUTS = [((16, 256, 128), 'float32')]


def kernel(**inputs):
    import numpy as _np
    import concourse.bacc as _bacc
    from concourse import mybir as _mybir
    from concourse.bass_utils import run_bass_kernel_spmd as _run

    nc = _bacc.Bacc("TRN2", target_bir_lowering=False, num_devices=1)
    arrays, args = {}, []
    for name in _INS:
        a = _np.ascontiguousarray(inputs[name])
        arrays[f"in_{name}_dram"] = a
        args.append(nc.dram_tensor(f"in_{name}_dram", a.shape, _mybir.dt.from_np(a.dtype), kind="ExternalInput").ap())
    for i, (shape, dtype) in enumerate(_OUTS):
        dt = _mybir.dt.from_np(_np.dtype(dtype))
        args.append(nc.dram_tensor(f"out_{i}_dram", shape, dt, kind="ExternalOutput").ap())
    two_block_kernel(nc, *args)
    r = _run(nc, [arrays], core_ids=[0])
    got = tuple(r.results[0][f"out_{i}_dram"] for i in range(len(_OUTS)))
    return got[0]
```

```python
from contextlib import ExitStack

import concourse.bass as bass
from concourse import mybir

F32 = mybir.dt.float32
BF16 = mybir.dt.bfloat16
I32 = mybir.dt.int32
U32 = mybir.dt.uint32
ALU = mybir.AluOpType
ACT = mybir.ActivationFunctionType
AX = mybir.AxisListType

P = 128
LN_EPS = 1e-5
ATT_EPS = 1e-6
NORM_EPS = 1e-9
LR = 0.01
RSQRT_SEED = 0x5F3759DF
EXP_FLOOR = -87.0

TILES = 4
LEVELS = 7
NEWTON = 3
LN_LINKS = 4 + 3 * NEWTON
GATE_LINKS = 15
JOINS_C = 3
CHAIN_A = LN_LINKS + GATE_LINKS + 2 + 1
CHAIN_B = LN_LINKS + 1 + 2
CHAIN_C = GATE_LINKS - 1 + 6 + 4
HALVES = 2
UNIT = HALVES * P
RING = 4
ROW = P + 2
COL_ID, COL_W = P, P + 1
CHOICES = 2


def two_block_kernel(nc, x, W_qkv, W_out, b_out, gate_w, w1_0, b1_0, w2_0, b2_0,
                     theta_K, theta_V, theta_Q, W0, b0, Wg, W1, b1, W2, b2, out):
    seqs, seq_len, D = x.shape
    E = gate_w.shape[1]
    HID0 = E * w1_0.shape[2]
    F = W1.shape[2]
    assert D == P and seq_len == 2 * P
    n_tiles = seqs * seq_len // P
    groups = n_tiles // TILES
    J0 = HID0 // P
    JF = F // P
    HT = E * JF
    tokens = n_tiles * P
    REGION = tokens + UNIT
    GROUP_SENDS = 16 * CHOICES * TILES
    GW = TILES * P
    RATE = 2.0 * LR / D

    x_rows = x.rearrange("s (h p) d -> p (s h) d", p=P)
    out_rows = out.rearrange("s (h p) d -> p (s h) d", p=P)

    routed = nc.dram_tensor("routed", (E * REGION, ROW), F32, kind="Internal").ap()
    results = nc.dram_tensor("results", (CHOICES * tokens + UNIT, D), F32, kind="Internal").ap()

    ctx = ExitStack()
    with ctx:
        def sb(name, shape, dt=F32):
            return ctx.enter_context(nc.sbuf_tensor(name, shape, dt))

        def bank(name):
            return ctx.enter_context(nc.psum_tensor(name, [P, 512], F32))

        def sem(name):
            return ctx.enter_context(nc.semaphore(name))

        x_all = sb("x_all", [P, n_tiles, D])
        w1_all = sb("w1_all", [P, E, F])
        w2_all = sb("w2_all", [P, HT, D])
        w1_l0 = sb("w1_l0", [P, E, HID0 // E])
        w2_l0 = sb("w2_l0", [P, J0, D])
        b2_l0 = sb("b2_l0", [E, D])
        gate0 = sb("gate0", [P, E])
        gate1 = sb("gate1", [P, E])
        nat = sb("nat", [P, 8, P])
        NAT_Q, NAT_K, NAT_V, NAT_OUT, NAT_TK, NAT_TV, NAT_TQ, NAT_W0 = range(8)
        b1_nat = sb("b1_nat", [HT + J0, P])
        rows = sb("rows", [1, 2 * D])
        b2_row = sb("b2_row", [1, E * D])
        b2_all = sb("b2_all", [P, E, D])
        wqT = sb("wqT", [P, P])
        wkT = sb("wkT", [P, P])
        woutT = sb("woutT", [P, P])
        wvo = sb("wvo", [P, P])
        tkT = sb("tkT", [P, P])
        tqT = sb("tqT", [P, P])
        tvT = sb("tvT", [P, P])
        w0T = sb("w0T", [P, P])
        m_res = sb("m_res", [P, P])
        m_out = sb("m_out", [P, P])
        b1T = sb("b1T", [P, HT + J0])
        bias_rows = sb("bias_rows", [P, 2, D])
        cb0 = sb("cb0", [P, D])

        ident = sb("ident", [P, P])
        ones_row = sb("ones_row", [1, P])
        mask_n = sb("mask_n", [P, P])
        mask_q = sb("mask_q", [P, P])
        mask_x = sb("mask_x", [P, TILES, P])
        mask_lv = sb("mask_lv", [P, LEVELS, P])
        expert_of = sb("expert_of", [E, J0, P], BF16)
        before = sb("before", [P, P], BF16)
        ones_b = sb("ones_b", [P, P], BF16)
        region0 = sb("region0", [P, E])
        ids = sb("ids", [P, CHOICES, n_tiles], I32)
        fill = sb("fill", [P, HALVES, ROW])
        rank_w = sb("rank_w", [P, TILES, E])

        stats = [sb(f"stats{b}", [P, TILES, 6]) for b in range(2)]
        mv = [sb(f"mv{b}", [P, TILES, 2]) for b in range(2)]
        v4 = [sb(f"v4{b}", [P, TILES]) for b in range(2)]
        seed = [sb(f"seed{b}", [P, TILES], I32) for b in range(2)]
        rstd = [sb(f"rstd{b}", [P, TILES]) for b in range(2)]
        nt_a = [sb(f"nt_a{b}", [P, TILES]) for b in range(2)]
        xn = sb("xn", [P, TILES, D])
        xnT0 = [sb(f"xnT0_{i}", [P, GW]) for i in range(2)]
        k0 = sb("k0", [P, TILES, D])
        v0 = sb("v0", [P, TILES, D + 1])
        q0T = sb("q0T", [P, GW])
        kv0 = sb("kv0", [P, TILES // 2, D + 1])
        z0 = sb("z0", [P, TILES])
        s0 = [sb(f"s0_{i}", [P, TILES, D]) for i in range(2)]

        def gate_scratch(b):
            names = ("d_lg", "th_lg", "num", "den", "ex", "tie", "first", "d2", "sel")
            return {**{n: sb(f"{n}{b}", [P, TILES, E]) for n in names},
                    **{n: sb(f"{n}{b}", [P, TILES]) for n in ("r4", "m4", "z4")}}

        gates = [gate_scratch(b) for b in range(2)]
        tok_w = [sb(f"tok_w_{i}", [P, TILES]) for i in range(2)]
        selT = [sb(f"selT_{i}", [E, GW]) for i in range(2)]
        selT_b = [sb(f"selT_b_{i}", [E, GW], BF16) for i in range(2)]
        h0T = sb("h0T", [P, J0, GW])
        hg0T = sb("hg0T", [P, J0, GW])
        gg0 = sb("gg0", [P, TILES, D])
        th0 = sb("th0", [P, TILES, D])
        mix = sb("mix", [P, TILES, D])

        xnT1 = [sb(f"xnT1_{i}", [P, GW]) for i in range(2)]

        pw = sb("pw", [P, TILES, E])
        sel_b = sb("sel_b", [P, TILES * E], BF16)
        place = sb("place", [P, TILES, E])
        pick = sb("pick", [P, 4, TILES, E])
        slot_f = sb("slot_f", [P, CHOICES, TILES])
        slot = [sb(f"slot_{i}", [P, CHOICES, TILES], U32) for i in range(2)]
        filled = sb("filled", [P, E])
        send = [[sb(f"send{i}_{c}", [P, TILES, ROW]) for c in range(CHOICES)] for i in range(2)]
        cnt_f = sb("cnt_f", [1, E])
        cnt_i = sb("cnt_i", [1, E], I32)
        units_i = sb("units_i", [1, E], I32)
        bound_f = sb("bound_f", [1, E + 1])
        table = sb("table", [1, 2 * E + 1], I32)

        kT = sb("kT", [P, GW])
        qT = sb("qT", [P, GW])
        raw = [sb(f"raw{i}", [P, TILES, P]) for i in range(2)]
        nT = [sb(f"nT_{i}", [P, TILES, P]) for i in range(2)]
        qkT = [sb(f"qkT_{i}", [P, TILES, P]) for i in range(2)]
        crossT = [sb(f"crossT_{i}", [P, TILES, P]) for i in range(2)]
        res = [sb(f"res_{i}", [P, TILES, D]) for i in range(2)]
        xinv = [sb(f"xinv_{i}", [P, TILES, P]) for i in range(2)]
        xinvT = [sb(f"xinvT_{i}", [P, TILES, P]) for i in range(2)]
        pn = [sb(f"pn{i}", [P, TILES, P]) for i in range(2)]
        upd = sb("upd", [P, TILES, D])
        res2 = sb("res2", [P, 2, D])
        s1 = sb("s1", [P, n_tiles, D])

        ring = sb("ring", [P, RING, HALVES, ROW])
        xu = sb("xu", [P, HALVES, D])
        xuT = sb("xuT", [P, UNIT])
        h1T = h0T[:, 0:JF, 0:UNIT]
        yb = sb("yb", [P, HALVES, D])
        yw = sb("yw", [P, HALVES, D])
        y_to = sb("y_to", [P, HALVES], U32)
        y_wt = sb("y_wt", [P, HALVES])
        th1 = [hg0T[:, i, :].rearrange("p (t d) -> p t d", t=TILES) for i in range(2)]
        mix2 = [hg0T[:, 2 + i, :].rearrange("p (t d) -> p t d", t=TILES) for i in range(2)]
        res_c = [w1_all[:, :, :].rearrange("p e (a d) -> p (e a) d", d=D), w2_all[:, :, :]]

        psA = [bank(f"psA{i}") for i in range(2)]
        psB = [bank(f"psB{i}") for i in range(2)]
        psC = [bank(f"psC{i}") for i in range(2)]
        psD = [bank(f"psD{i}") for i in range(2)]
        psH = [*psA, *psB]
        psX = psC[0]
        psY = psC[1]

        def tiles(ps):
            return ps[:, :].rearrange("p (t d) -> p t d", t=TILES)

        x_in = [sem(f"x_in{i}") for i in range(2)]
        w_small = sem("w_small")
        w_l0 = sem("w_l0")
        w_l1 = sem("w_l1")
        consts = sem("consts")
        pool_order = sem("pool_order")
        prep_ps = sem("prep_ps")
        prep_sb = sem("prep_sb")
        prep_dve = sem("prep_dve")
        count_order = sem("count_order")
        apart = sem("apart")
        table_ready = sem("table_ready")
        fill_in = sem("fill_in")
        res_in = [sem(f"res_in{g}") for g in range(groups)]
        order = {st: sem(f"order_{st}") for st in "ABC"}
        S = {n: sem(n) for n in (
            "stats0_ready", "stats1_ready", "xn0_ready", "xt0_ps", "xt0_ready", "k0_ps", "k0_ready", "v0_ps", "v0_ready", "q0_ps",
            "q0_ready", "lg0_ps", "lg0_read", "d0_ready", "tanh0_ready", "sel0_ready", "sel_ready", "kv0_ps",
            "kv0_ready", "att_ps", "z0_ready", "s0_raw", "s0_ready", "selT_ps", "selT_ready", "selTb_ready",
            "hid0_ps",
            "gelu0_ready",
            "selb_ps",
            "hg0_ready",
            "y0_ps", "gg0_ready", "silu0_ready", "x1_ready", "xn1_ready", "xt1_ps", "xt1_ready",
            "lg1_ps", "lg1_read", "sel1_ready", "d1_ready", "tanh1_ready", "pw_ready", "rank_ps", "rank_read",
            "slots_ready", "copy_sent",
            "rows_sent",
            "rows_landed",
            "kT_ps", "kT_ready", "qT_ps", "qT_ready", "n_ps", "n_ready", "qk_ps", "qk_ready",
            "cross_ps", "cross_ready", "res_ps", "res_ready",
            "qk_raw", "cross_raw", "res_raw", "s1_raw",
            *(f"xinv{lv}_ready" for lv in range(LEVELS - 1)),
            *(f"xinvT{lv}_ready" for lv in range(LEVELS)),
            "one_ready", *(f"join{lv}_ps" for lv in range(1, LEVELS)),
            *(f"p{lv}_ps" for lv in range(1, LEVELS)),
            *(f"p{lv}_ready" for lv in range(1, LEVELS)),
            "xt_ps",
            "u1_ps", "u1_ready", "res2_ps", "res2_ready", "u2_ps", "u2_ready", "o_ps",
            "s1_ready",
            "unit_in",
            "ring_free",
            "xu_ready", "xuT_ps", "xuT_ready",
            "hid_ps", "gelu_ready",
            "y_ps",
            "yb_ready",
            "yw_ready",
            "y_sent",
            "y_landed",
            "sum_ready", "mix_ready", "silu1_ready", "x2_ready", "x_out",
        )}

        SEEDED = {"s0_raw": 1, "s1_raw": 1, "lg1_read": 1, f"xinvT{JOINS_C}_ready": 1,
                  "rows_landed": 2}

        def wait_on(eng, name, value):
            eng.wait_ge(S[name], value + SEEDED.get(name, 0))

        LAG = {"A": 0, "B": 1, "C": 2, "D": 3}
        assert J0 == 4 and JOINS_C == 3 and LEVELS == 7
        PERIOD = (
            "C kT", "C landed", "C qT", "D half4", "A ln0", "B hid0 0", "C gram_q", "D join4",
            "A xt0", "C sel1", "C resid", "B hid0 1", "D half5", "C gram_n", "A lg0", "D join5",
            "B hid0 2", "A k", "C gram_x", "A sel0", "D turn", "B hid0 3", "C half1", "D half6",
            "C pw1", "A q", "C join1", "D join6", "A tok0", "B y0", "C rank", "B mix0", "C half2",
            "D u1", "A v", "D cross", "C join2", "A kv", "D u2", "A selT", "D out", "B ln1",
            "C half3", "A att", "C join3", "B xt1", "B lg1")

        def first_pass(eng, work):
            def period(p, par, stages="ABCD"):
                for entry in PERIOD:
                    stage, step = entry.split(" ", 1)
                    if stage in stages:
                        work(step, p - LAG[stage] if LAG[stage] else p, (par + LAG[stage]) % 2)

            period(0, 0, "A")
            period(1, 1, "AB")
            period(2, 0, "ABC")
            with eng.Fori(3, groups - 1, 2) as p:
                period(p, 1)
                period(p + 1, 0)
            period(groups - 1, 1)
            period(groups, 0, "BCD")
            period(groups + 1, 1, "CD")
            period(groups + 2, 0, "D")

        MAX_UNITS = (CHOICES * tokens) // UNIT + E

        def unit_bounds(eng):
            eng.wait_ge(table_ready, 1)
            return [eng.value_load(table[0:1, e:e + 1], min_val=0, max_val=MAX_UNITS)
                    for e in range(E + 1)]

        block = ctx.enter_context(nc.Block())

        @block.sync
        def _(sp):
            half = groups // 2
            sp.dma_start(x_all[:, 0:TILES, :], x_rows[:, 0:TILES, :]).then_inc(x_in[0], 16)
            for n, w in ((NAT_Q, W_qkv[0:D, :]), (NAT_K, W_qkv[D:2 * D, :]),
                         (NAT_V, W_qkv[2 * D:3 * D, :]), (NAT_OUT, W_out),
                         (NAT_TK, theta_K), (NAT_TV, theta_V), (NAT_TQ, theta_Q), (NAT_W0, W0)):
                sp.dma_start(nat[:, n, :], w).then_inc(w_small, 16)
            sp.dma_start(w1_l0[:, :, :], w1_0.rearrange("e d h -> d e h")).then_inc(w_l0, 16)
            sp.dma_start(w2_l0[:, :, :], w2_0.rearrange("e h d -> (e h) d")
                         .rearrange("(j p) d -> p j d", p=P)).then_inc(w_l0, 16)
            sp.dma_start(x_all[:, TILES:, :], x_rows[:, TILES:, :]).then_inc(x_in[1], 16)
            sp.dma_start(w1_all[:, :, :], W1.rearrange("e d f -> d e f")).then_inc(w_l1, 16)
            sp.dma_start(w2_all[:, :, :], W2.rearrange("e f d -> (e f) d")
                         .rearrange("(k p) d -> p k d", p=P)).then_inc(w_l1, 16)

            sp.sem_inc(S["unit_in"], 1)
            bounds = unit_bounds(sp)
            wait_on(sp, "rows_landed", groups)
            for e in range(E):
                free = sp.value_load(table[0:1, E + 1 + e:E + 2 + e], min_val=e * REGION,
                                     max_val=e * REGION + tokens)
                sp.dma_start(routed[bass.ds(free, UNIT), :].rearrange("(a p) d -> p a d", p=P),
                             fill[:, :, :]).then_inc(fill_in, 16)
            sp.wait_ge(fill_in, 16 * E)

            def load_unit(u, row):
                sp.wait_ge(S["unit_in"], u * 16 + 1)
                sp.sem_inc(apart, 1)
                sp.wait_ge(S["ring_free"], u + 1)
                sp.dma_start(ring[:, bass.ds(u % RING, 1), :, :].rearrange("p r a d -> p (r a) d"),
                             routed[bass.ds(row, UNIT), :].rearrange("(a p) d -> p a d", p=P)
                             ).then_inc(S["unit_in"], 16)

            for e in range(E):
                with sp.Fori(bounds[e], bounds[e + 1]) as u:
                    load_unit(u, nc.s_assert_within((u - bounds[e]) * UNIT + e * REGION,
                                                    e * REGION, e * REGION + tokens))
            load_unit(bounds[E], 0)

            sp.wait_ge(S["unit_in"], bounds[E] * 16 + 17)
            sp.wait_ge(S["y_landed"], bounds[E] + 1)
            sp.sem_inc(apart, 1)
            for g in range(groups):
                for c in range(CHOICES):
                    at = c * tokens + g * GW
                    sp.dma_start(res_c[c][:, g * TILES:(g + 1) * TILES, :],
                                 results[at:at + GW, :].rearrange("(t p) d -> p t d", p=P)
                                 ).then_inc(res_in[g], 16)
            for g in range(groups):
                sp.wait_ge(S["x2_ready"], g + 1)
                sp.dma_start(out_rows[:, g * TILES:(g + 1) * TILES, :],
                             x_all[:, g * TILES:(g + 1) * TILES, :]).then_inc(S["x_out"], 16)
            sp.wait_ge(S["x_out"], 16 * groups)

        @block.gpsimd
        def _(pool):
            done = [0]

            def ordered(ins):
                ins.then_inc(pool_order, 1)
                done[0] += 1
                pool.wait_ge(pool_order, done[0])

            ordered(pool.memset(ident[:, :], 0.0))
            pool.affine_select(out=ident[:, :], in_=ident[:, :], compare_op=ALU.not_equal, fill=1.0,
                               base=0, pattern=[[-1, P]], channel_multiplier=1).then_inc(consts, 1)
            pool.memset(ones_row[:, :], 1.0)
            pool.memset(v0[:, :, D:D + 1], 1.0)
            for e in range(E):
                pool.memset(rank_w[:, :, e:e + 1], float(E - e))
            pool.memset(mask_x[:, 0::2, :], -RATE)
            pool.memset(mask_x[:, 1::2, :], 1.0)
            for e in range(E):
                pool.memset(region0[:, e:e + 1], float(e * REGION))
            pool.memset(ones_b[:, :], 1.0)
            pool.memset(before[:, :], 1.0)
            pool.memset(fill[:, :, :], 0.0)
            for c in range(CHOICES):
                pool.iota(ids[:, c, :], pattern=[[P, n_tiles]], base=c * tokens, channel_multiplier=1)
            pool.memset(mask_n[:, :], -RATE)
            pool.memset(mask_q[:, :], 1.0)
            pool.memset(mask_lv[:, :, :], 0.0)
            ordered(pool.memset(expert_of[:, :, :], 0.0))
            pool.affine_select(out=mask_n[:, :], in_=mask_n[:, :], compare_op=ALU.is_gt, fill=0.0,
                               base=0, pattern=[[1, P]], channel_multiplier=-1)
            pool.affine_select(out=mask_q[:, :], in_=mask_q[:, :], compare_op=ALU.is_ge, fill=0.0,
                               base=0, pattern=[[1, P]], channel_multiplier=-1)
            pool.affine_select(out=before[:, :], in_=before[:, :], compare_op=ALU.is_gt, fill=0.0,
                               base=0, pattern=[[1, P]], channel_multiplier=-1)
            for a in range(HALVES):
                pool.iota(fill[:, a, COL_ID:COL_ID + 1].bitcast(I32), pattern=[[0, 1]],
                          base=CHOICES * tokens + a * P, channel_multiplier=1)
            eo = expert_of[:, :, :].rearrange("e j (a h) -> e (j a) h", h=HID0 // E)
            pool.affine_select(out=eo, in_=eo, compare_op=ALU.not_equal, fill=1.0,
                               base=0, pattern=[[-1, E], [0, HID0 // E]], channel_multiplier=1)
            for lv in range(LEVELS):
                b = 1 << lv
                odd = mask_lv[:, lv, :].rearrange("p (n a b) -> p n a b", a=2, b=b)[:, :, 1, :]
                ordered(pool.memset(odd, 1.0))
                ordered(pool.affine_select(out=odd, in_=odd, compare_op=ALU.is_ge, fill=0.0, base=0,
                                           pattern=[[-2 * b, P // (2 * b)], [0, b]],
                                           channel_multiplier=1))
                last = pool.affine_select(out=odd, in_=odd, compare_op=ALU.is_ge, fill=0.0,
                                          base=b - 1, pattern=[[2 * b, P // (2 * b)], [0, b]],
                                          channel_multiplier=-1)
            last.then_inc(consts, 1)
            pool.sem_inc(S["rows_landed"], SEEDED["rows_landed"])
            pool.sem_inc(S["y_landed"], 1)

            def work(step, g, par):
                def ready(*names):
                    for n in names:
                        wait_on(pool, n, g + 1)
                    pool.sem_inc(apart, 1)

                def four(m):
                    return m.unsqueeze(1).broadcast_to([P, TILES, P])

                group = bass.ds(g * TILES, TILES)
                if step == "kT":
                    ready("kT_ps")
                    pool.tensor_copy(xinvT[par][:, :, :], four(ident[:, :])).then_inc(S["one_ready"], 1)
                elif step == "landed" and not (isinstance(g, int) and g == 0):
                    pool.wait_ge(S["rows_sent"], g * GROUP_SENDS)
                    pool.sem_inc(S["rows_landed"], 1)
                elif step == "gram_q":
                    ready("qk_raw")
                    pool.tensor_tensor(qkT[par][:, :, :], raw[0][:, :, :], four(mask_q[:, :]),
                                       ALU.mult).then_inc(S["qk_ready"], 1)
                elif step == "gram_x":
                    ready("cross_raw")
                    pool.tensor_tensor(crossT[par][:, :, :], raw[1][:, :, :], mask_x[:, :, :],
                                       ALU.mult).then_inc(S["cross_ready"], 1)
                elif step == "resid":
                    ready("res_raw")
                    pool.tensor_tensor(res[par][:, :, :], res[par][:, :, :], four(cb0[:, :]),
                                       ALU.subtract).then_inc(S["res_ready"], 1)
                elif step == "rank":
                    ready("xn1_ready")
                    for c in range(CHOICES):
                        last = pool.tensor_copy(send[par][c][:, :, COL_ID:COL_ID + 1].bitcast(I32),
                                                ids[:, c, group].unsqueeze(2))
                    pool.tensor_copy(send[par][1][:, :, 0:D],
                                     send[par][0][:, :, 0:D]).then_inc(S["copy_sent"], 1)
                    ready("copy_sent", "slots_ready")
                    for t in range(TILES):
                        for c in range(CHOICES):
                            pool.indirect_dma_start(
                                routed[:, :], bass.IndirectOffsetOnAxis(ap=slot[par][:, c, t:t + 1], axis=0),
                                send[par][c][:, t, :], None).then_inc(S["rows_sent"], 16)
                elif step == "att":
                    ready("s0_raw")
                    pool.tensor_tensor(s0[par][:, :, :], s0[par][:, :, :], four(bias_rows[:, 0, :]),
                                       ALU.add).then_inc(S["s0_ready"], 1)
                elif step == "out":
                    ready("s1_raw")
                    pool.tensor_tensor(s1[:, group, :], s1[:, group, :],
                                       four(bias_rows[:, 1, :]), ALU.add).then_inc(S["s1_ready"], 1)

            first_pass(pool, work)
            pool.wait_ge(S["rows_sent"], groups * GROUP_SENDS)
            pool.sem_inc(S["rows_landed"], 1)

            bounds = unit_bounds(pool)
            with pool.Fori(0, bounds[E]) as u:
                pool.wait_ge(S["yw_ready"], u + 1)
                pool.sem_inc(apart, 1)
                for a in range(HALVES):
                    pool.indirect_dma_start(
                        results[:, :], bass.IndirectOffsetOnAxis(ap=y_to[:, a:a + 1], axis=0),
                        yw[:, a, :], None).then_inc(S["y_sent"], 16)
                pool.wait_ge(S["y_sent"], (u + 1) * (16 * HALVES))
                pool.sem_inc(S["y_landed"], 1)

            for g in range(groups):
                pool.wait_ge(S["sum_ready"], g + 1)
                if g >= 2:
                    pool.wait_ge(S["x2_ready"], g - 1)
                pool.wait_ge(S["s1_ready"], groups)
                pool.tensor_tensor(mix2[g % 2][:, :, :], s1[:, g * TILES:(g + 1) * TILES, :],
                                   res_c[0][:, g * TILES:(g + 1) * TILES, :],
                                   ALU.mult).then_inc(S["mix_ready"], 1)

        def load_small(act):
            act.dma_start(b1_nat[0:HT, :], b1.rearrange("e (j p) -> (e j) p", p=P)).then_inc(w_small, 16)
            act.dma_start(b1_nat[HT:HT + J0, :], b1_0.rearrange("e h -> (e h)")
                          .rearrange("(j p) -> j p", p=P)).then_inc(w_small, 16)
            act.dma_start(rows[:, 0:D], b_out.rearrange("(a n) -> a n", a=1)).then_inc(w_small, 16)
            act.dma_start(rows[:, D:2 * D], b0.rearrange("(a n) -> a n", a=1)).then_inc(w_small, 16)
            act.dma_start(gate0[:, :], gate_w).then_inc(w_small, 16)
            act.dma_start(gate1[:, :], Wg).then_inc(w_small, 16)
            act.dma_start(b2_l0[:, :], b2_0).then_inc(w_small, 16)
            act.dma_start(b2_row[:, :], b2.rearrange("(a e) d -> a (e d)", a=1)).then_inc(w_small, 16)

        SMALL_LOADS = 8 + 8

        @block.tensor
        def _(pe):
            mm = nc.tensor.matmul
            tr = nc.tensor.transpose

            pe.wait_ge(consts, 2)
            pe.wait_ge(w_small, 16 * SMALL_LOADS)
            for n, i in enumerate((NAT_Q, NAT_K, NAT_OUT, NAT_TK)):
                last = tr(psA[0][:, n * P:(n + 1) * P], nat[:, i, :], ident[:, :])
            last.then_inc(prep_ps, 1)
            for n, i in enumerate((NAT_TQ, NAT_TV, NAT_W0)):
                tr(psA[1][:, n * P:(n + 1) * P], nat[:, i, :], ident[:, :])
            tr(psA[1][:, 3 * P:3 * P + HT + J0], b1_nat[:, :],
               ident[0:HT + J0, 0:HT + J0]).then_inc(prep_ps, 1)
            mm(psB[0][:, 0:2 * D], ones_row[:, :], rows[:, :], start=True, stop=True).then_inc(prep_ps, 1)
            for n in range(2):
                mm(psC[n][:, :], ones_row[:, :], b2_row[:, n * 512:(n + 1) * 512],
                   start=True, stop=True)
            pe.wait_ge(prep_sb, 2)
            mm(psB[1][:, 0:P], nat[:, NAT_V, :], woutT[:, :], start=True, stop=True)
            mm(psB[1][:, P:2 * P], nat[:, NAT_TK, :], w0T[:, :], start=True, stop=True)
            mm(psB[1][:, 2 * P:3 * P], nat[:, NAT_TQ, :], w0T[:, :], start=True, stop=True).then_inc(prep_ps, 1)
            pe.wait_ge(prep_sb, 5)
            pe.wait_ge(w_l0, 32)

            def col(t):
                return slice(t * P, (t + 1) * P)

            def work(step, g, par):
                def ready(name, per=1, k=1):
                    wait_on(pe, name, g * per + k)

                h, xT0, xT = g, xnT0[par], xnT1[par]

                if step == "xt0":
                    ready("xn0_ready")
                    wait_on(pe, "s0_raw", g)
                    for t in range(TILES):
                        last = tr(psA[0][:, t * P:(t + 1) * P], xn[:, t, :], ident[:, :])
                    last.then_inc(S["xt0_ps"], 1)
                elif step == "lg0":
                    ready("xt0_ready")
                    for t in range(TILES):
                        last = mm(psA[1][:, t * E:(t + 1) * E], xT0[:, t * P:(t + 1) * P], gate0[:, :],
                                  start=True, stop=True)
                    last.then_inc(S["lg0_ps"], 1)
                elif step == "k":
                    for t in range(TILES):
                        last = mm(psA[0][:, t * P:(t + 1) * P], xT0[:, t * P:(t + 1) * P], wkT[:, :],
                                  start=True, stop=True)
                    last.then_inc(S["k0_ps"], 1)
                elif step == "v":
                    ready("lg0_read")
                    for t in range(TILES):
                        last = mm(psA[1][:, t * P:(t + 1) * P], xT0[:, t * P:(t + 1) * P], wvo[:, :],
                                  start=True, stop=True)
                    last.then_inc(S["v0_ps"], 1)
                elif step == "q":
                    ready("k0_ready")
                    mm(psA[0][:, :], wqT[:, :], xT0[:, :], start=True, stop=True).then_inc(S["q0_ps"], 1)
                elif step == "kv":
                    ready("v0_ready")
                    for s in range(2):
                        for t in range(2):
                            last = mm(psA[1][:, s * 256:s * 256 + D + 1], k0[:, 2 * s + t, :],
                                      v0[:, 2 * s + t, :], start=(t == 0), stop=(t == 1))
                    last.then_inc(S["kv0_ps"], 1)
                elif step == "selT":
                    ready("q0_ready")
                    ready("sel0_ready")
                    for t in range(TILES):
                        last = tr(psA[0][0:E, t * P:(t + 1) * P], gates[0]["sel"][:, t, :], ident[:, :])
                    last.then_inc(S["selT_ps"], 1)
                elif step == "att":
                    ready("kv0_ready")
                    ready("selTb_ready")
                    for t in range(TILES):
                        qt = q0T[:, t * P:(t + 1) * P]
                        mm(psA[0][:, t * P:(t + 1) * P], qt, kv0[:, t // 2, 0:D], start=True, stop=True)
                        last = mm(psA[1][:, t:t + 1], qt, kv0[:, t // 2, D:D + 1], start=True, stop=True)
                    last.then_inc(S["att_ps"], 1)
                elif step.startswith("hid0"):
                    j = int(step[4:])
                    if j == 0:
                        wait_on(pe, "lg1_read", g)
                        ready("selTb_ready")
                    else:
                        ready("hg0_ready", J0, j)
                    w = w1_l0[:, :, :].rearrange("d e h -> d (e h)")[:, j * P:(j + 1) * P]
                    mm(psB[0][:, :], w, xT0[:, :], start=True, stop=True).then_inc(S["hid0_ps"], 1)
                    mm(psB[1][:, :], expert_of[:, j, :], selT_b[par][:, :], start=True,
                       stop=True).then_inc(S["selb_ps"], 1)
                elif step == "y0":
                    ready("hg0_ready", J0, J0)
                    for t in range(TILES):
                        o = psB[0][:, t * P:(t + 1) * P]
                        for j in range(J0):
                            mm(o, hg0T[:, j, t * P:(t + 1) * P], w2_l0[:, j, :], start=(j == 0), stop=False)
                        last = mm(o, selT[par][:, t * P:(t + 1) * P], b2_l0[:, :], start=False, stop=True)
                    last.then_inc(S["y0_ps"], 1)
                elif step == "xt1":
                    ready("xn1_ready")
                    for t in range(TILES):
                        last = tr(psB[1][:, t * P:(t + 1) * P], send[par][0][:, t, 0:D], ident[:, :])
                    last.then_inc(S["xt1_ps"], 1)
                elif step == "lg1":
                    ready("gg0_ready")
                    ready("xt1_ready")
                    for t in range(TILES):
                        last = mm(psB[0][:, t * E:(t + 1) * E], xT[:, t * P:(t + 1) * P],
                                  gate1[:, :], start=True, stop=True)
                    last.then_inc(S["lg1_ps"], 1)
                elif step == "rank":
                    ready("pw_ready")
                    for t in range(TILES):
                        o = psB[1][:, t * E:(t + 1) * E]
                        mm(o, before[:, :], sel_b[:, t * E:(t + 1) * E], start=True, stop=(t == 0))
                        for s in range(t):
                            mm(o, ones_b[:, :], sel_b[:, s * E:(s + 1) * E], start=False,
                               stop=(s == t - 1))
                    for t in range(TILES):
                        last = mm(psB[1][:, TILES * E:TILES * E + E], ones_b[:, :],
                                  sel_b[:, t * E:(t + 1) * E], start=(t == 0), stop=(t == TILES - 1))
                    last.then_inc(S["rank_ps"], 1)

                elif step == "kT":
                    mm(psC[0][:, :], tkT[:, :], xT[:, :], start=True, stop=True).then_inc(S["kT_ps"], 1)
                elif step == "qT":
                    wait_on(pe, f"xinvT{JOINS_C}_ready", g)
                    mm(psC[1][:, :], tqT[:, :], xT[:, :], start=True, stop=True).then_inc(S["qT_ps"], 1)
                elif step == "gram_n":
                    ready("kT_ready")
                    for t in range(TILES):
                        last = mm(psC[0][:, col(t)], kT[:, col(t)], kT[:, col(t)], start=True, stop=True)
                    last.then_inc(S["n_ps"], 1)
                elif step == "gram_q":
                    ready("qT_ready")
                    for t in range(TILES):
                        last = mm(psC[1][:, col(t)], kT[:, col(t)], qT[:, col(t)], start=True, stop=True)
                    last.then_inc(S["qk_ps"], 1)
                elif step == "gram_x":
                    ready("n_ready")
                    for s in range(2):
                        a, b = col(2 * s), col(2 * s + 1)
                        mm(psC[0][:, a], kT[:, a], kT[:, b], start=True, stop=True)
                        last = mm(psC[0][:, b], kT[:, a], qT[:, b], start=True, stop=True)
                    last.then_inc(S["cross_ps"], 1)
                elif step == "resid":
                    ready("qk_raw")
                    for t in range(TILES):
                        last = mm(psC[1][:, col(t)], xT[:, col(t)], m_res[:, :], start=True, stop=True)
                    last.then_inc(S["res_ps"], 1)
                elif step.startswith("half"):
                    lv = int(step[4:])
                    bank = (psC if lv <= JOINS_C else psD)[0]
                    if lv == 1:
                        ready("cross_raw")
                    ready(f"xinv{lv - 1}_ready")
                    for t in range(TILES):
                        last = mm(bank[:, col(t)], nT[par][:, t, :], xinv[par][:, t, :], start=True,
                                  stop=True)
                    last.then_inc(S[f"p{lv}_ps"], 1)
                elif step.startswith("join"):
                    lv = int(step[4:])
                    c = 0 if lv <= JOINS_C else 1
                    if lv == 1:
                        ready("res_raw")
                    if lv == JOINS_C + 1:
                        wait_on(pe, "s1_raw", g)
                    ready(f"xinvT{lv - 1}_ready")
                    ready(f"p{lv}_ready")
                    for t in range(TILES):
                        last = mm((psC, psD)[c][1][:, col(t)], pn[c][:, t, :], xinvT[par][:, t, :],
                                  start=True, stop=True)
                    last.then_inc(S[f"join{lv}_ps"], 1)
                elif step == "turn":
                    ready(f"xinvT{LEVELS - 2}_ready")
                    for t in range(TILES):
                        last = tr(psD[0][:, col(t)], xinvT[par][:, t, :], ident[:, :])
                    last.then_inc(S["xt_ps"], 1)
                elif step == "u1":
                    ready(f"xinvT{LEVELS - 1}_ready")
                    ready("res_ready")
                    for t in (0, 2):
                        last = mm(psD[0][:, col(t)], xinvT[par][:, t, :], res[par][:, t, :], start=True, stop=True)
                    last.then_inc(S["u1_ps"], 1)
                elif step == "cross":
                    ready("u1_ready")
                    ready("cross_ready")
                    for s in range(2):
                        last = mm(psD[1][:, col(s)], crossT[par][:, 2 * s, :], upd[:, 2 * s, :],
                                  start=True, stop=True)
                    last.then_inc(S["res2_ps"], 1)
                elif step == "u2":
                    ready("res2_ready")
                    for s in range(2):
                        last = mm(psD[0][:, col(s)], xinvT[par][:, 2 * s + 1, :], res2[:, s, :],
                                  start=True, stop=True)
                    last.then_inc(S["u2_ps"], 1)
                elif step == "out":
                    ready("u2_ready")
                    ready("qk_ready")
                    for t in range(TILES):
                        o = psD[1][:, col(t)]
                        mm(o, xT[:, col(t)], m_out[:, :], start=True, stop=False)
                        if t % 2:
                            mm(o, crossT[par][:, t, :], upd[:, t - 1, :], start=False, stop=False)
                        last = mm(o, qkT[par][:, t, :], upd[:, t, :], start=False, stop=True)
                    last.then_inc(S["o_ps"], 1)

            first_pass(pe, work)

            pe.wait_ge(w_l1, 32)
            bounds = unit_bounds(pe)
            wait_on(pe, "s1_raw", groups)

            def turn(u):
                pe.wait_ge(S["xu_ready"], u + 1)
                for a in range(HALVES):
                    last = tr(psX[:, a * P:(a + 1) * P], xu[:, a, :], ident[:, :])
                last.then_inc(S["xuT_ps"], 1)

            turn(0)
            for e in range(E):
                with pe.Fori(bounds[e], bounds[e + 1]) as u:
                    pe.wait_ge(S["xuT_ready"], u + 1)
                    for j in range(JF):
                        mm(psH[j][:, 0:UNIT], w1_all[:, e, j * P:(j + 1) * P], xuT[:, :],
                           start=True, stop=True).then_inc(S["hid_ps"], 1)
                    turn(u + 1)
                    pe.wait_ge(S["yb_ready"], u + 1)
                    for a in range(HALVES):
                        for k in range(JF):
                            if a == 0:
                                pe.wait_ge(S["gelu_ready"], u * JF + k + 1)
                            last = mm(psY[:, a * P:(a + 1) * P], h1T[:, k, a * P:(a + 1) * P],
                                      w2_all[:, e * JF + k, :], start=(k == 0), stop=(k == JF - 1))
                    last.then_inc(S["y_ps"], 1)

        @block.scalar
        def _(act):
            load_small(act)
            f = nc.scalar.activation
            act.wait_ge(prep_ps, 1)
            for n, w in enumerate((wqT, wkT, woutT, tkT)):
                last = f(w[:, :], psA[0][:, n * P:(n + 1) * P], ACT.Copy)
            last.then_inc(prep_sb, 1)
            act.wait_ge(prep_ps, 2)
            for n, w in enumerate((tqT, tvT, w0T)):
                f(w[:, :], psA[1][:, n * P:(n + 1) * P], ACT.Copy)
            f(b1T[:, :], psA[1][:, 3 * P:3 * P + HT + J0], ACT.Copy).then_inc(prep_sb, 1)
            act.wait_ge(prep_ps, 3)
            f(bias_rows[:, :, :], psB[0][:, 0:2 * D].rearrange("p (a d) -> p a d", a=2),
              ACT.Copy).then_inc(prep_sb, 1)
            act.wait_ge(prep_sb, 3)
            f(cb0[:, :], bias_rows[:, 1, :], ACT.Copy, scale=RATE).then_inc(prep_sb, 1)
            act.wait_ge(prep_ps, 4)
            for n in range(2):
                f(b2_all[:, n * E // 2:(n + 1) * E // 2, :], tiles(psC[n]), ACT.Copy)
            f(wvo[:, :], psB[1][:, 0:P], ACT.Copy)
            f(m_out[:, :], psB[1][:, 2 * P:3 * P], ACT.Copy).then_inc(prep_dve, 1)

            act.sem_inc(S["s0_raw"], SEEDED["s0_raw"])
            act.sem_inc(S["s1_raw"], SEEDED["s1_raw"])

            def work(step, g, par):
                def ready(name, per=1, k=1):
                    wait_on(act, name, g * per + k)

                if step == "xt0":
                    ready("xt0_ps")
                    f(xnT0[par][:, :], psA[0][:, :], ACT.Copy).then_inc(S["xt0_ready"], 1)
                elif step == "v":
                    ready("v0_ps")
                    f(v0[:, :, 0:D], tiles(psA[1]), ACT.Copy).then_inc(S["v0_ready"], 1)
                elif step == "kv":
                    ready("kv0_ps")
                    f(kv0[:, :, :], psA[1][:, :].rearrange("p (s d) -> p s d", s=2)[:, :, 0:D + 1],
                      ACT.Copy).then_inc(S["kv0_ready"], 1)
                elif step in ("lg0", "lg1"):
                    b = int(step[2:])
                    ready(f"d{b}_ready")
                    f(gates[b]["th_lg"][:, :, :], gates[b]["d_lg"][:, :, :], ACT.Tanh,
                      scale=0.5).then_inc(S[f"tanh{b}_ready"], 1)
                elif step == "selT":
                    ready("selT_ps")
                    f(selT[par][:, :], psA[0][0:E, :], ACT.Copy)
                    f(selT_b[par][:, :], psA[0][0:E, :], ACT.Copy).then_inc(S["selTb_ready"], 1)
                elif step == "att":
                    ready("z0_ready")
                    for t in range(TILES):
                        last = f(s0[par][:, t, :], psA[0][:, t * P:(t + 1) * P], ACT.Copy,
                                 scale=z0[:, t:t + 1])
                    last.then_inc(S["s0_raw"], 1)
                elif step.startswith("hid0"):
                    j = int(step[4:])
                    ready("hid0_ps", J0, j + 1)
                    f(h0T[:, j, :], psB[0][:, :], ACT.Gelu,
                      bias=b1T[:, HT + j:HT + j + 1]).then_inc(S["gelu0_ready"], 1)
                elif step == "y0":
                    ready("y0_ps")
                    for t in range(TILES):
                        last = f(gg0[:, t, :], psB[0][:, t * P:(t + 1) * P], ACT.Copy,
                                 scale=tok_w[par][:, t:t + 1])
                    last.then_inc(S["gg0_ready"], 1)
                elif step == "mix0":
                    ready("gg0_ready")
                    f(th0[:, :, :], gg0[:, :, :], ACT.Tanh, scale=0.5).then_inc(S["silu0_ready"], 1)
                elif step == "xt1":
                    ready("xt1_ps")
                    f(xnT1[par][:, :], psB[1][:, :], ACT.Copy).then_inc(S["xt1_ready"], 1)
                elif step == "kT":
                    ready("kT_ps")
                    f(kT[:, :], psC[0][:, :], ACT.Copy).then_inc(S["kT_ready"], 1)
                elif step == "qT":
                    ready("qT_ps")
                    f(qT[:, :], psC[1][:, :], ACT.Copy).then_inc(S["qT_ready"], 1)
                elif step == "gram_q":
                    ready("one_ready")
                    ready("qk_ps")
                    f(raw[0][:, :, :], tiles(psC[1]), ACT.Copy, bias=1.0).then_inc(S["qk_raw"], 1)
                elif step == "gram_x":
                    ready("cross_ps")
                    f(raw[1][:, :, :], tiles(psC[0]), ACT.Copy, bias=1.0).then_inc(S["cross_raw"], 1)
                elif step == "resid":
                    ready("res_ps")
                    f(res[par][:, :, :], tiles(psC[1]), ACT.Copy).then_inc(S["res_raw"], 1)
                elif step.startswith("half"):
                    lv = int(step[4:])
                    c = 0 if lv <= JOINS_C else 1
                    ready(f"p{lv}_ps")
                    f(pn[c][:, :, :], tiles((psC, psD)[c][0]), ACT.Copy).then_inc(S[f"p{lv}_ready"], 1)
                elif step == "turn":
                    ready("xt_ps")
                    f(xinv[par][:, :, :], tiles(psD[0]), ACT.Copy).then_inc(S[f"xinv{LEVELS - 2}_ready"], 1)
                elif step == "u1":
                    ready("u1_ps")
                    f(upd[:, 0::2, :], tiles(psD[0])[:, 0::2, :], ACT.Copy).then_inc(S["u1_ready"], 1)
                elif step == "u2":
                    ready("u2_ps")
                    f(upd[:, 1::2, :], tiles(psD[0])[:, 0:2, :], ACT.Copy).then_inc(S["u2_ready"], 1)
                elif step == "out":
                    ready("o_ps")
                    act.sem_inc(apart, 1)
                    f(s1[:, bass.ds(g * TILES, TILES), :], tiles(psD[1]),
                      ACT.Copy).then_inc(S["s1_raw"], 1)

            first_pass(act, work)

            bounds = unit_bounds(act)

            def turned(u):
                act.wait_ge(S["xuT_ps"], u + 1)
                f(xuT[:, :], psX[:, 0:UNIT], ACT.Copy).then_inc(S["xuT_ready"], 1)

            turned(0)
            for e in range(E):
                with act.Fori(bounds[e], bounds[e + 1]) as u:
                    for j in range(JF):
                        n = e * JF + j
                        act.wait_ge(S["hid_ps"], u * JF + j + 1)
                        f(h1T[:, j, :], psH[j][:, 0:UNIT], ACT.Gelu,
                          bias=b1T[:, n:n + 1]).then_inc(S["gelu_ready"], 1)
                    turned(u + 1)
            for g in range(groups):
                act.wait_ge(S["sum_ready"], g + 1)
                if g >= 2:
                    act.wait_ge(S["x2_ready"], g - 1)
                f(th1[g % 2][:, :, :], res_c[0][:, g * TILES:(g + 1) * TILES, :], ACT.Tanh,
                  scale=0.5).then_inc(S["silu1_ready"], 1)

        @block.vector
        def _(dve):
            v = nc.vector
            links = dict.fromkeys("ABC", 0)
            CHAIN = {"A": CHAIN_A, "B": CHAIN_B, "C": CHAIN_C}

            def wait_apart(value, *signals):
                for s in signals:
                    dve.wait_ge(S[s], value)
                dve.sem_inc(apart, 1)

            dve.wait_ge(prep_dve, 1)
            v.tensor_tensor(m_res[:, :], tvT[:, :], psB[1][:, P:2 * P], ALU.subtract).then_inc(prep_dve, 1)
            dve.wait_ge(prep_dve, 2)
            v.tensor_scalar(m_res[:, :], m_res[:, :], RATE, None, ALU.mult).then_inc(prep_sb, 1)
            dve.wait_ge(consts, 2)
            dve.sem_inc(S["lg1_read"], SEEDED["lg1_read"])
            dve.sem_inc(S[f"xinvT{JOINS_C}_ready"], SEEDED[f"xinvT{JOINS_C}_ready"])
            dve.sem_inc(S["yb_ready"], 1)
            dve.sem_inc(S["ring_free"], RING)
            v.tensor_copy(filled[:, :], region0[:, :]).then_inc(prep_dve, 1)
            dve.wait_ge(prep_dve, 3)

            def bc(ap):
                return ap.unsqueeze(2).broadcast_to([P, TILES, E])

            def layer_norm(b, h, link, to):
                for t in range(TILES):
                    last = v.bn_stats(stats[b][:, t, :], x_all[:, bass.ds(h * TILES + t, 1), :])
                last.then_inc(S[f"stats{b}_ready"], 1)
                wait_apart(h + 1, f"stats{b}_ready")
                for t in range(TILES):
                    last = v.bn_aggr(mv[b][:, t, :], stats[b][:, t, :])
                link(last)
                r, a = rstd[b][:, :], nt_a[b][:, :]
                link(v.tensor_scalar(v4[b][:, :], mv[b][:, :, 1], LN_EPS, None, ALU.add))
                link(v.tensor_scalar(seed[b][:, :], v4[b][:, :].bitcast(I32), 1, None,
                                     ALU.logical_shift_right))
                link(v.tensor_scalar(r.bitcast(I32), seed[b][:, :], -1.0, float(RSQRT_SEED),
                                     ALU.mult, ALU.add))
                for _ in range(NEWTON):
                    link(v.scalar_tensor_tensor(a, r, -0.5, r, ALU.mult, ALU.mult))
                    link(v.tensor_tensor(a, a, v4[b][:, :], ALU.mult))
                    link(v.scalar_tensor_tensor(r, a, 1.5, r, ALU.add, ALU.mult))
                if b == 1:
                    wait_on(dve, "rows_landed", h - 1)
                for t in range(TILES):
                    last = v.tensor_scalar(to[:, t:t + 1, 0:D], x_all[:, bass.ds(h * TILES + t, 1), :],
                                           mv[b][:, t, 0:1], rstd[b][:, t:t + 1], ALU.subtract, ALU.mult)
                last.then_inc(S[f"xn{b}_ready"], 1)

            def shifted(b, ps, link, h):
                G = gates[b]
                lg = ps[:, 0:TILES * E].rearrange("p (t e) -> p t e", e=E)
                d = G["d_lg"][:, :, :]
                link(v.tensor_reduce(G["m4"][:, :], lg, AX.X, ALU.max))
                v.tensor_tensor(d, lg, bc(G["m4"][:, :]), ALU.subtract).then_inc(S[f"lg{b}_read"], 1)
                wait_on(dve, f"lg{b}_read", h + 1)
                v.tensor_scalar(d, d, EXP_FLOOR, None, ALU.max).then_inc(S[f"d{b}_ready"], 1)

            def two_largest(b, link, h):
                G = gates[b]
                d, tie, first, d2 = (G[n][:, :, :] for n in ("d_lg", "tie", "first", "d2"))
                wait_on(dve, f"d{b}_ready", h + 1)
                link(v.scalar_tensor_tensor(tie, d, 0.0, rank_w[:, :, :], ALU.is_equal, ALU.mult))
                link(v.tensor_reduce(G["r4"][:, :], tie, AX.X, ALU.max))
                link(v.tensor_tensor(first, tie, bc(G["r4"][:, :]), ALU.is_equal))
                link(v.scalar_tensor_tensor(d2, first, -1e30, d, ALU.mult, ALU.add))
                link(v.tensor_reduce(G["m4"][:, :], d2, AX.X, ALU.max))
                link(v.tensor_tensor(tie, d2, bc(G["m4"][:, :]), ALU.is_equal))
                link(v.tensor_tensor(tie, tie, rank_w[:, :, :], ALU.mult))
                link(v.tensor_reduce(G["r4"][:, :], tie, AX.X, ALU.max))
                link(v.tensor_tensor(tie, tie, bc(G["r4"][:, :]), ALU.is_equal))
                v.tensor_tensor(G["sel"][:, :, :], first, tie, ALU.add).then_inc(S[f"sel{b}_ready"], 1)

            def softmax(b, link, h):
                G = gates[b]
                th, num, den, ex = (G[n][:, :, :] for n in ("th_lg", "num", "den", "ex"))
                wait_on(dve, f"tanh{b}_ready", h + 1)
                v.tensor_scalar(num, th, 1.0, None, ALU.add)
                link(v.tensor_scalar(den, th, -1.0, 1.0, ALU.mult, ALU.add))
                link(v.reciprocal(den, den))
                link(v.tensor_tensor(ex, num, den, ALU.mult))
                link(v.tensor_reduce(G["z4"][:, :], ex, AX.X, ALU.add))
                link(v.reciprocal(G["z4"][:, :], G["z4"][:, :]))

            def work(step, g, par):
                def ready(name, per=1, k=1):
                    wait_on(dve, name, g * per + k)

                def link_in(stage):
                    def link(ins):
                        ins.then_inc(order[stage], 1)
                        links[stage] += 1
                        dve.wait_ge(order[stage], g * CHAIN[stage] + links[stage])
                    return link

                def four(m):
                    return m.unsqueeze(1).broadcast_to([P, TILES, P])

                in_a, in_b, in_c = link_in("A"), link_in("B"), link_in("C")
                if step == "ln0":
                    links["A"] = 0
                    layer_norm(0, g, in_a, xn)
                elif step == "lg0":
                    ready("lg0_ps")
                    shifted(0, psA[1], in_a, g)
                elif step == "sel0":
                    two_largest(0, in_a, g)
                elif step == "tok0":
                    softmax(0, in_a, g)
                    G = gates[0]
                    ready("sel0_ready")
                    in_a(v.tensor_tensor(G["ex"][:, :, :], G["ex"][:, :, :], G["sel"][:, :, :], ALU.mult))
                    in_a(v.tensor_reduce(G["m4"][:, :], G["ex"][:, :, :], AX.X, ALU.add))
                    v.tensor_tensor(tok_w[par][:, :], G["m4"][:, :], G["z4"][:, :],
                                    ALU.mult).then_inc(S["sel_ready"], 1)
                elif step == "k":
                    ready("k0_ps")
                    v.tensor_scalar(k0[:, :, :], tiles(psA[0]), 0.0, ATT_EPS, ALU.max,
                                    ALU.add).then_inc(S["k0_ready"], 1)
                elif step == "q":
                    ready("q0_ps")
                    v.tensor_scalar(q0T[:, :], psA[0][:, :], 0.0, ATT_EPS, ALU.max,
                                    ALU.add).then_inc(S["q0_ready"], 1)
                elif step == "att":
                    ready("att_ps")
                    in_a(v.tensor_scalar(z0[:, :], psA[1][:, 0:TILES], ATT_EPS, None, ALU.add))
                    v.reciprocal(z0[:, :], z0[:, :]).then_inc(S["z0_ready"], 1)
                    assert links["A"] == CHAIN_A, links
                elif step.startswith("hid0"):
                    j = int(step[4:])
                    ready("gelu0_ready", J0, j + 1)
                    ready("selb_ps", J0, j + 1)
                    v.tensor_tensor(hg0T[:, j, :], h0T[:, j, :], psB[1][:, :],
                                    ALU.mult).then_inc(S["hg0_ready"], 1)
                elif step == "mix0":
                    links["B"] = 0
                    ready("s0_ready")
                    ready("gg0_ready")
                    in_b(v.tensor_tensor(mix[:, :, :], s0[par][:, :, :], gg0[:, :, :], ALU.mult))
                    ready("silu0_ready")
                    in_b(v.scalar_tensor_tensor(mix[:, :, :], th0[:, :, :], 1.0, mix[:, :, :],
                                                ALU.add, ALU.mult))
                    xg = x_all[:, bass.ds(g * TILES, TILES), :]
                    v.scalar_tensor_tensor(xg, mix[:, :, :], 0.5, xg, ALU.mult,
                                           ALU.add).then_inc(S["x1_ready"], 1)
                elif step == "ln1":
                    wait_apart(g + 1, "x1_ready")
                    layer_norm(1, g, in_b, send[par][0])
                elif step == "lg1":
                    ready("lg1_ps")
                    shifted(1, psB[0], in_b, g)
                    assert links["B"] == CHAIN_B, links
                elif step == "sel1":
                    links["C"] = 0
                    two_largest(1, in_c, g)
                elif step == "pw1":
                    softmax(1, in_c, g)
                    G = gates[1]
                    ex, m4 = G["ex"][:, :, :], G["m4"][:, :]
                    in_c(v.tensor_tensor(ex, ex, bc(G["z4"][:, :]), ALU.mult))
                    ready("sel1_ready")
                    v.tensor_copy(sel_b[:, :].rearrange("p (t e) -> p t e", e=E), G["sel"][:, :, :])
                    in_c(v.tensor_tensor(ex, ex, G["sel"][:, :, :], ALU.mult))
                    in_c(v.tensor_reduce(m4, ex, AX.X, ALU.add))
                    in_c(v.tensor_scalar(m4, m4, NORM_EPS, None, ALU.add))
                    in_c(v.reciprocal(m4, m4))
                    v.tensor_tensor(pw[:, :, :], ex, bc(m4), ALU.mult).then_inc(S["pw_ready"], 1)
                    ready("pw_ready")
                    v.tensor_tensor(pick[:, 0], G["first"][:, :, :], pw[:, :, :], ALU.mult)
                    in_c(v.tensor_tensor(pick[:, 1], G["tie"][:, :, :], pw[:, :, :], ALU.mult))
                    for c in range(CHOICES):
                        v.tensor_reduce(send[par][c][:, :, COL_W], pick[:, c], AX.X, ALU.add)
                elif step == "rank":
                    G = gates[1]
                    ready("rank_ps")
                    in_c(v.tensor_tensor(place[:, :, :],
                                         psB[1][:, 0:TILES * E].rearrange("p (t e) -> p t e", e=E),
                                         filled[:, :].unsqueeze(1).broadcast_to([P, TILES, E]), ALU.add))
                    in_c(v.tensor_tensor(filled[:, :], filled[:, :],
                                         psB[1][:, TILES * E:TILES * E + E], ALU.add))
                    v.tensor_tensor(pick[:, 2], G["first"][:, :, :], place[:, :, :], ALU.mult)
                    in_c(v.tensor_tensor(pick[:, 3], G["tie"][:, :, :], place[:, :, :], ALU.mult))
                    for c in range(CHOICES):
                        last = v.tensor_reduce(slot_f[:, c, :], pick[:, 2 + c], AX.X, ALU.add)
                    in_c(last)
                    v.tensor_copy(slot[par][:, :, :], slot_f[:, :, :]).then_inc(S["slots_ready"], 1)
                    assert links["C"] == CHAIN_C, links
                elif step == "gram_n":
                    ready("n_ps")
                    v.scalar_tensor_tensor(nT[par][:, :, :], tiles(psC[0]), 1.0, four(mask_n[:, :]),
                                           ALU.add, ALU.mult).then_inc(S["n_ready"], 1)
                    wait_apart(g + 1, "one_ready", "n_ready")
                    v.copy_predicated(xinvT[par][:, :, :], four(mask_lv[:, 0, :].bitcast(I32)),
                                      nT[par][:, :, :]).then_inc(S["xinvT0_ready"], 1)
                    ready("xinvT0_ready")
                    v.transpose(xinv[par][:, :, :], xinvT[par][:, :, :]).then_inc(S["xinv0_ready"], 1)
                elif step.startswith("join"):
                    lv = int(step[4:])
                    wait_apart(g + 1, f"join{lv}_ps")
                    v.copy_predicated(xinvT[par][:, :, :], four(mask_lv[:, lv, :].bitcast(I32)),
                                      tiles((psC if lv <= JOINS_C else psD)[1])
                                      ).then_inc(S[f"xinvT{lv}_ready"], 1)
                    if lv < LEVELS - 2:
                        ready(f"xinvT{lv}_ready")
                        v.transpose(xinv[par][:, :, :], xinvT[par][:, :, :]
                                    ).then_inc(S[f"xinv{lv}_ready"], 1)
                elif step == "cross":
                    ready("res2_ps")
                    v.tensor_tensor(res2[:, :, :], tiles(psD[1])[:, 0:2, :], res[par][:, 1::2, :],
                                    ALU.add).then_inc(S["res2_ready"], 1)

            dve.wait_ge(x_in[0], 16)
            dve.wait_ge(x_in[1], 16)
            first_pass(dve, work)

            counted = [0]

            def then(ins):
                ins.then_inc(count_order, 1)
                counted[0] += 1
                dve.wait_ge(count_order, counted[0])

            then(v.tensor_tensor(cnt_f[:, :], filled[0:1, :], region0[0:1, :], ALU.subtract))
            then(v.tensor_scalar(cnt_i[:, :], cnt_f[:, :], float(UNIT - 1), None, ALU.add))
            then(v.tensor_scalar(units_i[:, :], cnt_i[:, :], UNIT.bit_length() - 1, None,
                                 ALU.logical_shift_right))
            then(v.tensor_scalar(cnt_f[:, :], units_i[:, :], 1.0, None, ALU.max))
            then(v.memset(bound_f[:, 0:1], 0.0))
            for e in range(E):
                then(v.tensor_tensor(bound_f[:, e + 1:e + 2], bound_f[:, e:e + 1],
                                     cnt_f[:, e:e + 1], ALU.add))
            v.tensor_copy(table[:, E + 1:2 * E + 1], filled[0:1, :])
            v.tensor_copy(table[:, 0:E + 1], bound_f[:, :]).then_inc(table_ready, 1)

            bounds = unit_bounds(dve)

            def take(u):
                dve.wait_ge(S["unit_in"], u * 16 + 17)
                v.tensor_scalar(xu[:, :, :],
                                ring[:, bass.ds(u % RING, 1), :, 0:D].rearrange("p r a d -> p (r a) d"),
                                1.0, None, ALU.mult).then_inc(S["xu_ready"], 1)

            take(0)
            for e in range(E):
                with dve.Fori(bounds[e], bounds[e + 1]) as u:
                    dve.wait_ge(S["xuT_ps"], u + 1)
                    take(u + 1)
                    dve.wait_ge(S["y_ps"], u + 1)
                    v.tensor_tensor(yb[:, :, :], psY[:, 0:UNIT].rearrange("p (a d) -> p a d", a=HALVES),
                                    b2_all[:, e, :].unsqueeze(1).broadcast_to([P, HALVES, D]),
                                    ALU.add).then_inc(S["yb_ready"], 1)
                    dve.wait_ge(S["y_landed"], u + 1)
                    at = ring[:, bass.ds(u % RING, 1), :, :]
                    v.tensor_scalar(y_to[:, :].unsqueeze(2),
                                    at[:, :, :, COL_ID:COL_ID + 1].bitcast(I32)
                                    .rearrange("p r a d -> p (r a) d"), 0.0, None, ALU.add)
                    v.tensor_scalar(y_wt[:, :].unsqueeze(2), at[:, :, :, COL_W:COL_W + 1]
                                    .rearrange("p r a d -> p (r a) d"), 1.0, None,
                                    ALU.mult).then_inc(S["ring_free"], 1)
                    dve.wait_ge(S["ring_free"], u + 1 + RING)
                    dve.wait_ge(S["yb_ready"], u + 2)
                    for a in range(HALVES):
                        last = v.tensor_scalar(yw[:, a, :], yb[:, a, :], y_wt[:, a:a + 1], None,
                                               ALU.mult)
                    last.then_inc(S["yw_ready"], 1)

            def finish(g):
                ts = slice(g * TILES, (g + 1) * TILES)
                m = mix2[g % 2][:, :, :]
                dve.wait_ge(S["mix_ready"], g + 1)
                dve.wait_ge(S["silu1_ready"], g + 1)
                v.scalar_tensor_tensor(m, th1[g % 2][:, :, :], 1.0, m, ALU.add,
                                       ALU.mult).then_inc(count_order, 1)
                dve.wait_ge(count_order, counted[0] + g + 1)
                v.scalar_tensor_tensor(x_all[:, ts, :], m, 0.5, x_all[:, ts, :], ALU.mult,
                                       ALU.add).then_inc(S["x2_ready"], 1)

            for g in range(groups):
                ts = slice(g * TILES, (g + 1) * TILES)
                dve.wait_ge(res_in[g], 16 * CHOICES)
                v.tensor_tensor(res_c[0][:, ts, :], res_c[0][:, ts, :], res_c[1][:, ts, :],
                                ALU.add).then_inc(S["sum_ready"], 1)
                if g:
                    finish(g - 1)
            finish(groups - 1)


_INS = ['L0_attn_x', 'L0_attn_W_qkv', 'L0_attn_W_out', 'L0_attn_b_out', 'L0_ffn_gate_w', 'L0_ffn_w1',
        'L0_ffn_b1', 'L0_ffn_w2', 'L0_ffn_b2', 'L1_attn_theta_K', 'L1_attn_theta_V',
        'L1_attn_theta_Q', 'L1_attn_W0', 'L1_attn_b0', 'L1_ffn_Wg', 'L1_ffn_W1', 'L1_ffn_b1',
        'L1_ffn_W2', 'L1_ffn_b2']
_OUTS = [((16, 256, 128), 'float32')]


def kernel(**inputs):
    import numpy as _np
    import concourse.bacc as _bacc
    from concourse import mybir as _mybir
    from concourse.bass_utils import run_bass_kernel_spmd as _run

    nc = _bacc.Bacc("TRN2", target_bir_lowering=False, num_devices=1)
    arrays, args = {}, []
    for name in _INS:
        a = _np.ascontiguousarray(inputs[name])
        arrays[f"in_{name}_dram"] = a
        args.append(nc.dram_tensor(f"in_{name}_dram", a.shape, _mybir.dt.from_np(a.dtype), kind="ExternalInput").ap())
    for i, (shape, dtype) in enumerate(_OUTS):
        dt = _mybir.dt.from_np(_np.dtype(dtype))
        args.append(nc.dram_tensor(f"out_{i}_dram", shape, dt, kind="ExternalOutput").ap())
    two_block_kernel(nc, *args)
    r = _run(nc, [arrays], core_ids=[0])
    got = tuple(r.results[0][f"out_{i}_dram"] for i in range(len(_OUTS)))
    return got[0]
```

```python
from contextlib import ExitStack

import concourse.bass as bass
from concourse import mybir

F32 = mybir.dt.float32
BF16 = mybir.dt.bfloat16
I32 = mybir.dt.int32
U32 = mybir.dt.uint32
ALU = mybir.AluOpType
ACT = mybir.ActivationFunctionType
AX = mybir.AxisListType

P = 128
LN_EPS = 1e-5
ATT_EPS = 1e-6
NORM_EPS = 1e-9
LR = 0.01
RSQRT_SEED = 0x5F3759DF
EXP_FLOOR = -87.0

TILES = 4
LEVELS = 7
NEWTON = 3
LN_LINKS = 4 + 3 * NEWTON
GATE_LINKS = 15
JOINS_C = 3
CHAIN_A = LN_LINKS + GATE_LINKS + 2 + 1
CHAIN_B = LN_LINKS + 1 + 2
CHAIN_C = GATE_LINKS - 1 + 6 + 4
HALVES = 2
UNIT = HALVES * P
RING = 4
ROW = P + 2
COL_ID, COL_W = P, P + 1
CHOICES = 2


def two_block_kernel(nc, x, W_qkv, W_out, b_out, gate_w, w1_0, b1_0, w2_0, b2_0,
                     theta_K, theta_V, theta_Q, W0, b0, Wg, W1, b1, W2, b2, out):
    seqs, seq_len, D = x.shape
    E = gate_w.shape[1]
    HID0 = E * w1_0.shape[2]
    F = W1.shape[2]
    assert D == P and seq_len == 2 * P
    n_tiles = seqs * seq_len // P
    groups = n_tiles // TILES
    J0 = HID0 // P
    JF = F // P
    HT = E * JF
    tokens = n_tiles * P
    REGION = tokens + UNIT
    MIN_UNITS = 3
    FILLINGS = 6
    GROUP_SENDS = 16 * CHOICES * TILES
    GW = TILES * P
    RATE = 2.0 * LR / D

    x_rows = x.rearrange("s (h p) d -> p (s h) d", p=P)
    out_rows = out.rearrange("s (h p) d -> p (s h) d", p=P)

    routed = nc.dram_tensor("routed", (E * REGION, ROW), F32, kind="Internal").ap()
    results = nc.dram_tensor("results", (CHOICES * tokens + FILLINGS * UNIT, D), F32, kind="Internal").ap()

    ctx = ExitStack()
    with ctx:
        def sb(name, shape, dt=F32):
            return ctx.enter_context(nc.sbuf_tensor(name, shape, dt))

        def bank(name):
            return ctx.enter_context(nc.psum_tensor(name, [P, 512], F32))

        def sem(name):
            return ctx.enter_context(nc.semaphore(name))

        x_all = sb("x_all", [P, n_tiles, D])
        w1_all = sb("w1_all", [P, E, F])
        w2_all = sb("w2_all", [P, HT, D])
        w1_l0 = sb("w1_l0", [P, E, HID0 // E])
        w2_l0 = sb("w2_l0", [P, J0, D])
        b2_l0 = sb("b2_l0", [E, D])
        gate0 = sb("gate0", [P, E])
        gate1 = sb("gate1", [P, E])
        nat = sb("nat", [P, 8, P])
        NAT_Q, NAT_K, NAT_V, NAT_OUT, NAT_TK, NAT_TV, NAT_TQ, NAT_W0 = range(8)
        b1_nat = sb("b1_nat", [HT + J0, P])
        rows = sb("rows", [1, 2 * D])
        b2_row = sb("b2_row", [1, E * D])
        b2_all = sb("b2_all", [P, E, D])
        wqT = sb("wqT", [P, P])
        wkT = sb("wkT", [P, P])
        woutT = sb("woutT", [P, P])
        wvo = sb("wvo", [P, P])
        tkT = sb("tkT", [P, P])
        tqT = sb("tqT", [P, P])
        tvT = sb("tvT", [P, P])
        w0T = sb("w0T", [P, P])
        m_res = sb("m_res", [P, P])
        m_out = sb("m_out", [P, P])
        b1T = sb("b1T", [P, HT + J0])
        bias_rows = sb("bias_rows", [P, 2, D])
        cb0 = sb("cb0", [P, D])

        ident = sb("ident", [P, P])
        ones_row = sb("ones_row", [1, P])
        mask_n = sb("mask_n", [P, P])
        mask_q = sb("mask_q", [P, P])
        mask_x = sb("mask_x", [P, TILES, P])
        mask_lv = sb("mask_lv", [P, LEVELS, P])
        expert_of = sb("expert_of", [E, J0, P], BF16)
        before = sb("before", [P, P], BF16)
        ones_b = sb("ones_b", [P, P], BF16)
        region0 = sb("region0", [P, E])
        ids = sb("ids", [P, CHOICES, n_tiles], I32)
        fill = sb("fill", [P, 2, HALVES, ROW])
        rank_w = sb("rank_w", [P, TILES, E])

        stats = [sb(f"stats{b}", [P, TILES, 6]) for b in range(2)]
        mv = [sb(f"mv{b}", [P, TILES, 2]) for b in range(2)]
        v4 = [sb(f"v4{b}", [P, TILES]) for b in range(2)]
        seed = [sb(f"seed{b}", [P, TILES], I32) for b in range(2)]
        rstd = [sb(f"rstd{b}", [P, TILES]) for b in range(2)]
        nt_a = [sb(f"nt_a{b}", [P, TILES]) for b in range(2)]
        xn = sb("xn", [P, TILES, D])
        xnT0 = [sb(f"xnT0_{i}", [P, GW]) for i in range(2)]
        k0 = sb("k0", [P, TILES, D])
        v0 = sb("v0", [P, TILES, D + 1])
        q0T = sb("q0T", [P, GW])
        kv0 = sb("kv0", [P, TILES // 2, D + 1])
        z0 = sb("z0", [P, TILES])
        s0 = [sb(f"s0_{i}", [P, TILES, D]) for i in range(2)]

        def gate_scratch(b):
            names = ("d_lg", "th_lg", "num", "den", "ex", "tie", "first", "d2", "sel")
            return {**{n: sb(f"{n}{b}", [P, TILES, E]) for n in names},
                    **{n: sb(f"{n}{b}", [P, TILES]) for n in ("r4", "m4", "z4")}}

        gates = [gate_scratch(b) for b in range(2)]
        tok_w = [sb(f"tok_w_{i}", [P, TILES]) for i in range(2)]
        selT = [sb(f"selT_{i}", [E, GW]) for i in range(2)]
        selT_b = [sb(f"selT_b_{i}", [E, GW], BF16) for i in range(2)]
        h0T = sb("h0T", [P, J0, GW])
        hg0T = sb("hg0T", [P, J0, GW])
        gg0 = sb("gg0", [P, TILES, D])
        th0 = sb("th0", [P, TILES, D])
        mix = sb("mix", [P, TILES, D])

        xnT1 = [sb(f"xnT1_{i}", [P, GW]) for i in range(2)]

        pw = sb("pw", [P, TILES, E])
        sel_b = sb("sel_b", [P, TILES * E], BF16)
        place = sb("place", [P, TILES, E])
        pick = sb("pick", [P, 4, TILES, E])
        slot_f = sb("slot_f", [P, CHOICES, TILES])
        slot = [sb(f"slot_{i}", [P, CHOICES, TILES], U32) for i in range(2)]
        filled = sb("filled", [P, E])
        send = [[sb(f"send{i}_{c}", [P, TILES, ROW]) for c in range(CHOICES)] for i in range(2)]
        cnt_f = sb("cnt_f", [1, E])
        cnt_i = sb("cnt_i", [1, E], I32)
        units_i = sb("units_i", [1, E], I32)
        bound_f = sb("bound_f", [1, E + 1])
        table = sb("table", [1, 2 * E + 2], I32)

        kT = sb("kT", [P, GW])
        qT = sb("qT", [P, GW])
        raw = [sb(f"raw{i}", [P, TILES, P]) for i in range(2)]
        nT = [sb(f"nT_{i}", [P, TILES, P]) for i in range(2)]
        qkT = [sb(f"qkT_{i}", [P, TILES, P]) for i in range(2)]
        crossT = [sb(f"crossT_{i}", [P, TILES, P]) for i in range(2)]
        res = [sb(f"res_{i}", [P, TILES, D]) for i in range(2)]
        xinv = [sb(f"xinv_{i}", [P, TILES, P]) for i in range(2)]
        xinvT = [sb(f"xinvT_{i}", [P, TILES, P]) for i in range(2)]
        pn = [sb(f"pn{i}", [P, TILES, P]) for i in range(2)]
        upd = sb("upd", [P, TILES, D])
        res2 = sb("res2", [P, 2, D])
        s1 = sb("s1", [P, n_tiles, D])

        ring = sb("ring", [P, RING, HALVES, ROW])
        xu = sb("xu", [P, HALVES, D])
        xuT = sb("xuT", [P, UNIT])
        h1T = h0T[:, 0:JF, 0:UNIT]
        yw = nat[:, 0:2 * HALVES, :].rearrange("p (i a) d -> p i a d", i=2)
        yb = nat[:, 2 * HALVES:3 * HALVES, :]
        y_to = sb("y_to", [P, 2, HALVES], U32)
        y_wt = sb("y_wt", [P, HALVES])
        th1 = [hg0T[:, i, :].rearrange("p (t d) -> p t d", t=TILES) for i in range(2)]
        mix2 = [hg0T[:, 2 + i, :].rearrange("p (t d) -> p t d", t=TILES) for i in range(2)]
        res_c = [w1_all[:, :, :].rearrange("p e (a d) -> p (e a) d", d=D), w2_all[:, :, :]]

        psA = [bank(f"psA{i}") for i in range(2)]
        psB = [bank(f"psB{i}") for i in range(2)]
        psC = [bank(f"psC{i}") for i in range(2)]
        psD = [bank(f"psD{i}") for i in range(2)]
        psH = psA
        psX = psB[0]
        psY = [psB[1], psC[0]]

        def tiles(ps):
            return ps[:, :].rearrange("p (t d) -> p t d", t=TILES)

        x_in = [sem(f"x_in{i}") for i in range(2)]
        w_small = sem("w_small")
        w_l0 = sem("w_l0")
        w_l1 = sem("w_l1")
        consts = sem("consts")
        pool_order = sem("pool_order")
        prep_ps = sem("prep_ps")
        prep_sb = sem("prep_sb")
        prep_dve = sem("prep_dve")
        count_order = sem("count_order")
        apart = sem("apart")
        table_ready = sem("table_ready")
        fill_in = sem("fill_in")
        prefilled = sem("prefilled")
        ring_given = sem("ring_given")
        all_landed = sem("all_landed")
        res_in = [sem(f"res_in{g}") for g in range(groups)]
        order = {st: sem(f"order_{st}") for st in "ABC"}
        S = {n: sem(n) for n in (
            "stats0_ready", "stats1_ready", "xn0_ready", "xt0_ps", "xt0_ready", "k0_ps", "k0_ready", "v0_ps", "v0_ready", "q0_ps",
            "q0_ready", "lg0_ps", "lg0_read", "d0_ready", "tanh0_ready", "sel0_ready", "sel_ready", "kv0_ps",
            "kv0_ready", "att_ps", "z0_ready", "s0_raw", "s0_ready", "selT_ps", "selTb_ready",
            "hid0_ps",
            "gelu0_ready",
            "selb_ps",
            "hg0_ready",
            "y0_ps", "gg0_ready", "silu0_ready", "x1_ready", "xn1_ready", "xt1_ps", "xt1_ready",
            "lg1_ps", "lg1_read", "sel1_ready", "d1_ready", "tanh1_ready", "pw_ready", "rank_ps",
            "slots_ready", "copy_sent",
            "rows_sent",
            "rows_landed",
            "kT_ps", "kT_ready", "qT_ps", "qT_ready", "n_ps", "n_ready", "qk_ps", "qk_ready",
            "cross_ps", "cross_ready", "res_ps", "res_ready",
            "qk_raw", "cross_raw", "res_raw", "s1_raw",
            *(f"xinv{lv}_ready" for lv in range(LEVELS - 1)),
            *(f"xinvT{lv}_ready" for lv in range(LEVELS)),
            "one_ready", *(f"join{lv}_ps" for lv in range(1, LEVELS)),
            *(f"p{lv}_ps" for lv in range(1, LEVELS)),
            *(f"p{lv}_ready" for lv in range(1, LEVELS)),
            "xt_ps",
            "u1_ps", "u1_ready", "res2_ps", "res2_ready", "u2_ps", "u2_ready", "o_ps",
            "s1_ready",
            "unit_in",
            "ring_free",
            "xu_ready", "xuT_ps", "xuT_ready",
            "hid_ps",
            "gelu_ready",
            "h1_free",
            "yb_ready",
            "yw_ready",
            "y_sent0", "y_sent1",
            "y_landed",
            "sum_ready", "mix_ready", "silu1_ready", "x2_ready", "x_out",
        )}

        SEEDED = {"s0_raw": 1, "s1_raw": 1, "lg1_read": 1, f"xinvT{JOINS_C}_ready": 1,
                  "rows_landed": 2,
                  "yb_ready": 1, "y_landed": 2, "unit_in": 1, "ring_free": RING, "h1_free": JF,
                  "gelu_ready": JF, "yw_ready": 1}

        def wait_on(eng, name, value):
            eng.wait_ge(S[name], value + SEEDED.get(name, 0))

        def blocks(m, lv, odd):
            return m.rearrange("p t (n a b) -> p t n a b", a=2, b=1 << lv)[:, :, :, odd, :]

        def packed(ps, lv):
            return ps[:, 0:TILES * P // 2].rearrange("p (t n b) -> p t n b", t=TILES, b=1 << lv)

        LAG = {"A": 0, "B": 1, "C": 2, "D": 3}
        assert J0 == 4 and JOINS_C == 3 and LEVELS == 7
        PERIOD = (
            "C kT", "D half4", "C qT", "C one", "A ln0", "B hid0 0", "D join4", "C gram_n",
            "A xt0", "C gram_q", "B hid0 1", "A lg0", "C copies", "D half5", "C sel1", "B hid0 2",
            "C resid", "D join5", "C pw1", "C gram_x", "B hid0 3", "D turn", "A sel0", "A tok0",
            "C half1", "D half6", "C join1", "B y0", "C landed", "C rank", "A k", "D join6",
            "B mix0", "C half2", "A v", "C join2", "D u1", "A q", "D cross", "A kv", "C half3",
            "D u2", "B ln1", "A selT", "C join3", "D out", "B xt1", "A att", "B lg1")

        CLOSE = (
            "C kT", "C one", "C landed", "C copies", "C sel1", "C qT", "D half4", "C gram_n",
            "C pw1", "D join4", "C gram_q", "C rank", "D half5", "C resid", "C gram_x", "U sent",
            "D join5", "C half1", "D turn", "C join1", "D half6", "C half2", "D join6",
            "C join2", "D u1", "C half3", "D cross", "C join3", "D u2", "D out", "E half4",
            "E join4", "U first", "E half5", "U hid 0", "E join5", "E turn", "U gelu 0",
            "U hid 1", "E half6", "U out 0", "E join6", "U hid 2", "E u1", "U out 1", "E cross",
            "U hid 3", "E u2", "U out 2", "E out", "U hid 4", "U out 3", "U hid 5", "U out 4",
            "U hid 6", "U out 5", "U hid 7", "U out 6")
        assert E == 8

        def first_pass(eng, work, unit_work):
            def period(p, par, stages="ABCD"):
                for entry in PERIOD:
                    stage, step = entry.split(" ", 1)
                    if stage in stages:
                        work(step, p - LAG[stage] if LAG[stage] else p, (par + LAG[stage]) % 2)

            period(0, 0, "A")
            period(1, 1, "AB")
            period(2, 0, "ABC")
            with eng.Fori(3, groups - 1, 2) as p:
                period(p, 1)
                period(p + 1, 0)
            period(groups - 1, 1)
            period(groups, 0, "BCD")
            for entry in CLOSE:
                stage, step = entry.split(" ", 1)
                if stage == "U":
                    what, *k = step.split()
                    unit_work(what, *map(int, k))
                else:
                    g = groups - 2 if stage == "D" else groups - 1
                    work(step, g, g % 2)

        MAX_UNITS = (CHOICES * tokens) // UNIT + MIN_UNITS * E

        def unit_bounds(eng, first=0, last=E + 1):
            eng.wait_ge(table_ready, 1)
            return [eng.value_load(table[0:1, e:e + 1], min_val=E, max_val=MAX_UNITS)
                    for e in range(first, last)]

        def other_units(eng, bounds, hid, out):
            for e in range(E):
                hid(bounds[e], e)
                out(bounds[e] - 1, e - 1 if e else E - 1, e)
                with eng.Fori(bounds[e] + 1, bounds[e + 1]) as u:
                    hid(u, e)
                    out(u - 1, e, e)
            out(bounds[E] - 1, E - 1, None)

        block = ctx.enter_context(nc.Block())

        @block.sync
        def _(sp):
            half = groups // 2
            sp.dma_start(x_all[:, 0:TILES, :], x_rows[:, 0:TILES, :]).then_inc(x_in[0], 16)
            for n, w in ((NAT_Q, W_qkv[0:D, :]), (NAT_K, W_qkv[D:2 * D, :]),
                         (NAT_V, W_qkv[2 * D:3 * D, :]), (NAT_OUT, W_out),
                         (NAT_TK, theta_K), (NAT_TV, theta_V), (NAT_TQ, theta_Q), (NAT_W0, W0)):
                sp.dma_start(nat[:, n, :], w).then_inc(w_small, 16)
            sp.dma_start(w1_l0[:, :, :], w1_0.rearrange("e d h -> d e h")).then_inc(w_l0, 16)
            sp.dma_start(w2_l0[:, :, :], w2_0.rearrange("e h d -> (e h) d")
                         .rearrange("(j p) d -> p j d", p=P)).then_inc(w_l0, 16)
            sp.dma_start(x_all[:, TILES:, :], x_rows[:, TILES:, :]).then_inc(x_in[1], 16)
            sp.dma_start(w1_all[:, :, :], W1.rearrange("e d f -> d e f")).then_inc(w_l1, 16)
            sp.dma_start(w2_all[:, :, :], W2.rearrange("e f d -> (e f) d")
                         .rearrange("(k p) d -> p k d", p=P)).then_inc(w_l1, 16)

            sp.wait_ge(consts, 2)
            for e in range(E):
                for n in range(MIN_UNITS):
                    at = e * REGION + n * UNIT
                    sp.dma_start(routed[at:at + UNIT, :].rearrange("(a p) d -> p a d", p=P),
                                 ring[:, n + 1 if n else e % 2, :, :]).then_inc(prefilled, 16)
            sp.wait_ge(prefilled, 16 * E * MIN_UNITS)
            sp.sem_inc(ring_given, 1)

            sp.sem_inc(S["unit_in"], SEEDED["unit_in"])
            bounds = unit_bounds(sp)
            free = [sp.value_load(table[0:1, E + 1 + e:E + 2 + e], min_val=e * REGION,
                                  max_val=e * REGION + tokens) for e in range(E)]
            wait_on(sp, "rows_landed", groups)
            for e in range(E):
                sp.dma_start(routed[bass.ds(free[e], UNIT), :].rearrange("(a p) d -> p a d", p=P),
                             fill[:, e % 2, :, :]).then_inc(fill_in, 16)
            sp.wait_ge(fill_in, 16 * E)

            def load_unit(u, row):
                wait_on(sp, "unit_in", u * 16)
                sp.sem_inc(apart, 1)
                wait_on(sp, "ring_free", u - RING + 1)
                sp.dma_start(ring[:, bass.ds(u % RING, 1), :, :].rearrange("p r a d -> p (r a) d"),
                             routed[bass.ds(row, UNIT), :].rearrange("(a p) d -> p a d", p=P)
                             ).then_inc(S["unit_in"], 16)

            for e in range(E):
                load_unit(e, e * REGION)
            for e in range(E):
                with sp.Fori(bounds[e], bounds[e + 1]) as u:
                    load_unit(u, nc.s_assert_within((u - bounds[e] + 1) * UNIT + e * REGION,
                                                    e * REGION, e * REGION + tokens))
            load_unit(bounds[E], 0)
            load_unit(bounds[E] + 1, 0)

            wait_on(sp, "unit_in", (bounds[E] + 2) * 16)
            sp.sem_inc(apart, 1)
            sp.wait_ge(all_landed, 1)
            for g in range(groups):
                for c in range(CHOICES):
                    at = c * tokens + g * GW
                    sp.dma_start(res_c[c][:, g * TILES:(g + 1) * TILES, :],
                                 results[at:at + GW, :].rearrange("(t p) d -> p t d", p=P)
                                 ).then_inc(res_in[g], 16)
            for g in range(groups):
                sp.wait_ge(S["x2_ready"], g + 1)
                sp.dma_start(out_rows[:, g * TILES:(g + 1) * TILES, :],
                             x_all[:, g * TILES:(g + 1) * TILES, :]).then_inc(S["x_out"], 16)
            sp.wait_ge(S["x_out"], 16 * groups)

        @block.gpsimd
        def _(pool):
            done = [0]

            def ordered(ins):
                ins.then_inc(pool_order, 1)
                done[0] += 1
                pool.wait_ge(pool_order, done[0])

            pool.memset(ones_row[:, :], 1.0)
            ordered(pool.memset(ident[:, :], 0.0))
            pool.affine_select(out=ident[:, :], in_=ident[:, :], compare_op=ALU.not_equal, fill=1.0,
                               base=0, pattern=[[-1, P]], channel_multiplier=1).then_inc(consts, 1)
            pool.memset(v0[:, :, D:D + 1], 1.0)
            for e in range(E):
                pool.memset(rank_w[:, :, e:e + 1], float(E - e))
            pool.memset(mask_x[:, 0::2, :], -RATE)
            pool.memset(mask_x[:, 1::2, :], 1.0)
            for e in range(E):
                pool.memset(region0[:, e:e + 1], float(e * REGION))
            pool.memset(ones_b[:, :], 1.0)
            pool.memset(before[:, :], 1.0)
            pool.memset(fill[:, :, :, :], 0.0)
            pool.memset(ring[:, :, :, :], 0.0)
            for c in range(2):
                pool.memset(pn[c][:, :, :], 0.0)
            for c in range(CHOICES):
                pool.iota(ids[:, c, :], pattern=[[P, n_tiles]], base=c * tokens, channel_multiplier=1)
            pool.memset(mask_n[:, :], -RATE)
            pool.memset(mask_q[:, :], 1.0)
            pool.memset(mask_lv[:, :, :], 0.0)
            ordered(pool.memset(expert_of[:, :, :], 0.0))
            pool.affine_select(out=mask_n[:, :], in_=mask_n[:, :], compare_op=ALU.is_gt, fill=0.0,
                               base=0, pattern=[[1, P]], channel_multiplier=-1)
            pool.affine_select(out=mask_q[:, :], in_=mask_q[:, :], compare_op=ALU.is_ge, fill=0.0,
                               base=0, pattern=[[1, P]], channel_multiplier=-1)
            pool.affine_select(out=before[:, :], in_=before[:, :], compare_op=ALU.is_gt, fill=0.0,
                               base=0, pattern=[[1, P]], channel_multiplier=-1)
            for n in range(FILLINGS):
                for a in range(HALVES):
                    at = (fill[:, n, a, COL_ID:COL_ID + 1] if n < 2 else
                          ring[:, n - 2, a, COL_ID:COL_ID + 1])
                    pool.iota(at.bitcast(I32), pattern=[[0, 1]], channel_multiplier=1,
                              base=CHOICES * tokens + (n * HALVES + a) * P)
            eo = expert_of[:, :, :].rearrange("e j (a h) -> e (j a) h", h=HID0 // E)
            pool.affine_select(out=eo, in_=eo, compare_op=ALU.not_equal, fill=1.0,
                               base=0, pattern=[[-1, E], [0, HID0 // E]], channel_multiplier=1)
            for lv in range(LEVELS):
                b = 1 << lv
                odd = mask_lv[:, lv, :].rearrange("p (n a b) -> p n a b", a=2, b=b)[:, :, 1, :]
                ordered(pool.memset(odd, 1.0))
                ordered(pool.affine_select(out=odd, in_=odd, compare_op=ALU.is_ge, fill=0.0, base=0,
                                           pattern=[[-2 * b, P // (2 * b)], [0, b]],
                                           channel_multiplier=1))
                last = pool.affine_select(out=odd, in_=odd, compare_op=ALU.is_ge, fill=0.0,
                                          base=b - 1, pattern=[[2 * b, P // (2 * b)], [0, b]],
                                          channel_multiplier=-1)
            last.then_inc(consts, 1)
            pool.sem_inc(S["rows_landed"], SEEDED["rows_landed"])
            pool.sem_inc(S["y_landed"], SEEDED["y_landed"])

            def work(step, g, par):
                def ready(*names):
                    for n in names:
                        wait_on(pool, n, g + 1)
                    pool.sem_inc(apart, 1)

                def four(m):
                    return m.unsqueeze(1).broadcast_to([P, TILES, P])

                group = bass.ds(g * TILES, TILES)
                if step == "one":
                    ready("kT_ps")
                    pool.tensor_copy(xinvT[par][:, :, :], four(ident[:, :])).then_inc(S["one_ready"], 1)
                elif step == "landed" and not (isinstance(g, int) and g == 0):
                    pool.wait_ge(S["rows_sent"], g * GROUP_SENDS)
                    pool.sem_inc(S["rows_landed"], 1)
                elif step == "gram_q":
                    ready("qk_raw")
                    pool.tensor_tensor(qkT[par][:, :, :], raw[0][:, :, :], four(mask_q[:, :]),
                                       ALU.mult).then_inc(S["qk_ready"], 1)
                elif step == "gram_x":
                    ready("cross_raw")
                    pool.tensor_tensor(crossT[par][:, :, :], raw[1][:, :, :], mask_x[:, :, :],
                                       ALU.mult).then_inc(S["cross_ready"], 1)
                elif step == "resid":
                    ready("res_raw")
                    pool.tensor_tensor(res[par][:, :, :], res[par][:, :, :], four(cb0[:, :]),
                                       ALU.subtract).then_inc(S["res_ready"], 1)
                elif step == "copies":
                    ready("xn1_ready")
                    for c in range(CHOICES):
                        last = pool.tensor_copy(send[par][c][:, :, COL_ID:COL_ID + 1].bitcast(I32),
                                                ids[:, c, group].unsqueeze(2))
                    pool.tensor_copy(send[par][1][:, :, 0:D],
                                     send[par][0][:, :, 0:D]).then_inc(S["copy_sent"], 1)
                elif step == "rank":
                    if isinstance(g, int) and g == 0:
                        pool.wait_ge(ring_given, 1)
                    ready("copy_sent", "slots_ready")
                    for t in range(TILES):
                        for c in range(CHOICES):
                            pool.indirect_dma_start(
                                routed[:, :], bass.IndirectOffsetOnAxis(ap=slot[par][:, c, t:t + 1], axis=0),
                                send[par][c][:, t, :], None).then_inc(S["rows_sent"], 16)
                elif step == "att":
                    ready("s0_raw")
                    pool.tensor_tensor(s0[par][:, :, :], s0[par][:, :, :], four(bias_rows[:, 0, :]),
                                       ALU.add).then_inc(S["s0_ready"], 1)
                elif step == "out":
                    ready("s1_raw")
                    pool.tensor_tensor(s1[:, group, :], s1[:, group, :],
                                       four(bias_rows[:, 1, :]), ALU.add).then_inc(S["s1_ready"], 1)

            def send_results(u, par):
                wait_on(pool, "yw_ready", u + 1)
                pool.sem_inc(apart, 1)
                for a in range(HALVES):
                    pool.indirect_dma_start(
                        results[:, :], bass.IndirectOffsetOnAxis(ap=y_to[:, par, a:a + 1], axis=0),
                        yw[:, par, a, :], None).then_inc(S[f"y_sent{par}"], 16)
                if not (isinstance(u, int) and u == 0):
                    pool.wait_ge(S[f"y_sent{1 - par}"], (u + par) * (8 * HALVES))
                    pool.sem_inc(S["y_landed"], 1)

            def unit_work(what, k=0):
                if what == "sent":
                    pool.wait_ge(S["rows_sent"], groups * GROUP_SENDS)
                    pool.sem_inc(S["rows_landed"], 1)
                elif what == "out":
                    send_results(k, k % 2)

            first_pass(pool, work, unit_work)
            send_results(E - 1, 1)
            pool.wait_ge(table_ready, 1)
            pairs_end = pool.value_load(table[0:1, 2 * E + 1:2 * E + 2], min_val=E,
                                        max_val=MAX_UNITS + 1)
            with pool.Fori(E, pairs_end, 2) as u:
                send_results(u, 0)
                send_results(u + 1, 1)
            pool.wait_ge(S["y_sent1"], pairs_end * (8 * HALVES))
            pool.sem_inc(all_landed, 1)

            for g in range(groups):
                pool.wait_ge(S["sum_ready"], g + 1)
                if g >= 2:
                    pool.wait_ge(S["x2_ready"], g - 1)
                pool.wait_ge(S["s1_ready"], groups)
                pool.tensor_tensor(mix2[g % 2][:, :, :], s1[:, g * TILES:(g + 1) * TILES, :],
                                   res_c[0][:, g * TILES:(g + 1) * TILES, :],
                                   ALU.mult).then_inc(S["mix_ready"], 1)

        def load_small(act):
            act.dma_start(b1_nat[0:HT, :], b1.rearrange("e (j p) -> (e j) p", p=P)).then_inc(w_small, 16)
            act.dma_start(b1_nat[HT:HT + J0, :], b1_0.rearrange("e h -> (e h)")
                          .rearrange("(j p) -> j p", p=P)).then_inc(w_small, 16)
            act.dma_start(rows[:, 0:D], b_out.rearrange("(a n) -> a n", a=1)).then_inc(w_small, 16)
            act.dma_start(rows[:, D:2 * D], b0.rearrange("(a n) -> a n", a=1)).then_inc(w_small, 16)
            act.dma_start(gate0[:, :], gate_w).then_inc(w_small, 16)
            act.dma_start(gate1[:, :], Wg).then_inc(w_small, 16)
            act.dma_start(b2_l0[:, :], b2_0).then_inc(w_small, 16)
            act.dma_start(b2_row[:, :], b2.rearrange("(a e) d -> a (e d)", a=1)).then_inc(w_small, 16)

        SMALL_LOADS = 8 + 8

        @block.tensor
        def _(pe):
            mm = nc.tensor.matmul
            tr = nc.tensor.transpose

            pe.wait_ge(consts, 1)
            pe.wait_ge(w_small, 16 * SMALL_LOADS)
            for n, i in enumerate((NAT_Q, NAT_K, NAT_OUT, NAT_TK)):
                last = tr(psA[0][:, n * P:(n + 1) * P], nat[:, i, :], ident[:, :])
            last.then_inc(prep_ps, 1)
            for n, i in enumerate((NAT_TQ, NAT_TV, NAT_W0)):
                tr(psA[1][:, n * P:(n + 1) * P], nat[:, i, :], ident[:, :])
            tr(psA[1][:, 3 * P:3 * P + HT + J0], b1_nat[:, :],
               ident[0:HT + J0, 0:HT + J0]).then_inc(prep_ps, 1)
            mm(psB[0][:, 0:2 * D], ones_row[:, :], rows[:, :], start=True, stop=True).then_inc(prep_ps, 1)
            for n in range(2):
                mm(psC[n][:, :], ones_row[:, :], b2_row[:, n * 512:(n + 1) * 512],
                   start=True, stop=True)
            pe.wait_ge(prep_sb, 2)
            mm(psB[1][:, 0:P], nat[:, NAT_V, :], woutT[:, :], start=True, stop=True)
            mm(psB[1][:, P:2 * P], nat[:, NAT_TK, :], w0T[:, :], start=True, stop=True)
            mm(psB[1][:, 2 * P:3 * P], nat[:, NAT_TQ, :], w0T[:, :], start=True, stop=True).then_inc(prep_ps, 1)
            pe.wait_ge(prep_sb, 5)
            pe.wait_ge(consts, 2)
            pe.wait_ge(w_l0, 32)
            pe.sem_inc(S["h1_free"], SEEDED["h1_free"])

            def col(t):
                return slice(t * P, (t + 1) * P)

            def work(step, g, par):
                def ready(name, per=1, k=1):
                    wait_on(pe, name, g * per + k)

                h, xT0, xT = g, xnT0[par], xnT1[par]

                if step == "xt0":
                    ready("xn0_ready")
                    wait_on(pe, "s0_raw", g)
                    for t in range(TILES):
                        last = tr(psA[0][:, t * P:(t + 1) * P], xn[:, t, :], ident[:, :])
                    last.then_inc(S["xt0_ps"], 1)
                elif step == "lg0":
                    ready("xt0_ready")
                    for t in range(TILES):
                        last = mm(psA[1][:, t * E:(t + 1) * E], xT0[:, t * P:(t + 1) * P], gate0[:, :],
                                  start=True, stop=True)
                    last.then_inc(S["lg0_ps"], 1)
                elif step == "k":
                    for t in range(TILES):
                        last = mm(psA[0][:, t * P:(t + 1) * P], xT0[:, t * P:(t + 1) * P], wkT[:, :],
                                  start=True, stop=True)
                    last.then_inc(S["k0_ps"], 1)
                elif step == "v":
                    ready("lg0_read")
                    for t in range(TILES):
                        last = mm(psA[1][:, t * P:(t + 1) * P], xT0[:, t * P:(t + 1) * P], wvo[:, :],
                                  start=True, stop=True)
                    last.then_inc(S["v0_ps"], 1)
                elif step == "q":
                    ready("k0_ready")
                    mm(psA[0][:, :], wqT[:, :], xT0[:, :], start=True, stop=True).then_inc(S["q0_ps"], 1)
                elif step == "kv":
                    ready("v0_ready")
                    for s in range(2):
                        for t in range(2):
                            last = mm(psA[1][:, s * 256:s * 256 + D + 1], k0[:, 2 * s + t, :],
                                      v0[:, 2 * s + t, :], start=(t == 0), stop=(t == 1))
                    last.then_inc(S["kv0_ps"], 1)
                elif step == "selT":
                    ready("q0_ready")
                    ready("sel0_ready")
                    for t in range(TILES):
                        last = tr(psA[0][0:E, t * P:(t + 1) * P], gates[0]["sel"][:, t, :], ident[:, :])
                    last.then_inc(S["selT_ps"], 1)
                elif step == "att":
                    ready("kv0_ready")
                    ready("selTb_ready")
                    for t in range(TILES):
                        qt = q0T[:, t * P:(t + 1) * P]
                        last = mm(psA[t // 2][:, (t % 2) * 256:(t % 2) * 256 + D + 1], qt,
                                  kv0[:, t // 2, :], start=True, stop=True)
                    last.then_inc(S["att_ps"], 1)
                elif step.startswith("hid0"):
                    j = int(step[4:])
                    if j == 0:
                        wait_on(pe, "lg1_read", g)
                        ready("selTb_ready")
                    else:
                        ready("hg0_ready", J0, j)
                    w = w1_l0[:, :, :].rearrange("d e h -> d (e h)")[:, j * P:(j + 1) * P]
                    mm(psB[0][:, :], w, xT0[:, :], start=True, stop=True).then_inc(S["hid0_ps"], 1)
                    mm(psB[1][:, :], expert_of[:, j, :], selT_b[par][:, :], start=True,
                       stop=True).then_inc(S["selb_ps"], 1)
                elif step == "y0":
                    ready("hg0_ready", J0, J0)
                    for t in range(TILES):
                        o = psB[0][:, t * P:(t + 1) * P]
                        for j in range(J0):
                            mm(o, hg0T[:, j, t * P:(t + 1) * P], w2_l0[:, j, :], start=(j == 0), stop=False)
                        last = mm(o, selT[par][:, t * P:(t + 1) * P], b2_l0[:, :], start=False, stop=True)
                    last.then_inc(S["y0_ps"], 1)
                elif step == "xt1":
                    ready("xn1_ready")
                    for t in range(TILES):
                        last = tr(psB[1][:, t * P:(t + 1) * P], send[par][0][:, t, 0:D], ident[:, :])
                    last.then_inc(S["xt1_ps"], 1)
                elif step == "lg1":
                    ready("gg0_ready")
                    ready("xt1_ready")
                    for t in range(TILES):
                        last = mm(psB[0][:, t * E:(t + 1) * E], xT[:, t * P:(t + 1) * P],
                                  gate1[:, :], start=True, stop=True)
                    last.then_inc(S["lg1_ps"], 1)
                elif step == "rank":
                    ready("pw_ready")
                    for t in range(TILES):
                        o = psB[1][:, t * E:(t + 1) * E]
                        mm(o, before[:, :], sel_b[:, t * E:(t + 1) * E], start=True, stop=(t == 0))
                        for s in range(t):
                            mm(o, ones_b[:, :], sel_b[:, s * E:(s + 1) * E], start=False,
                               stop=(s == t - 1))
                    for t in range(TILES):
                        last = mm(psB[1][:, TILES * E:TILES * E + E], ones_b[:, :],
                                  sel_b[:, t * E:(t + 1) * E], start=(t == 0), stop=(t == TILES - 1))
                    last.then_inc(S["rank_ps"], 1)

                elif step == "kT":
                    mm(psC[0][:, :], tkT[:, :], xT[:, :], start=True, stop=True).then_inc(S["kT_ps"], 1)
                elif step == "qT":
                    wait_on(pe, f"xinvT{JOINS_C}_ready", g)
                    mm(psC[1][:, :], tqT[:, :], xT[:, :], start=True, stop=True).then_inc(S["qT_ps"], 1)
                elif step == "gram_n":
                    ready("kT_ready")
                    for t in range(TILES):
                        last = mm(psC[0][:, col(t)], kT[:, col(t)], kT[:, col(t)], start=True, stop=True)
                    last.then_inc(S["n_ps"], 1)
                elif step == "gram_q":
                    ready("qT_ready")
                    for t in range(TILES):
                        last = mm(psC[1][:, col(t)], kT[:, col(t)], qT[:, col(t)], start=True, stop=True)
                    last.then_inc(S["qk_ps"], 1)
                elif step == "gram_x":
                    ready("n_ready")
                    for s in range(2):
                        a, b = col(2 * s), col(2 * s + 1)
                        mm(psC[0][:, a], kT[:, a], kT[:, b], start=True, stop=True)
                        last = mm(psC[0][:, b], kT[:, a], qT[:, b], start=True, stop=True)
                    last.then_inc(S["cross_ps"], 1)
                elif step == "resid":
                    ready("qk_raw")
                    for t in range(TILES):
                        last = mm(psC[1][:, col(t)], xT[:, col(t)], m_res[:, :], start=True, stop=True)
                    last.then_inc(S["res_ps"], 1)
                elif step.startswith("half"):
                    lv = int(step[4:])
                    bank = (psC if lv <= JOINS_C else psD)[0]
                    if lv == 1:
                        ready("cross_raw")
                    ready(f"xinv{lv - 1}_ready")
                    for t in range(TILES):
                        last = mm(packed(bank, lv)[:, t], nT[par][:, t, :],
                                  blocks(xinv[par], lv, 0)[:, t], start=True, stop=True)
                    last.then_inc(S[f"p{lv}_ps"], 1)
                elif step.startswith("join"):
                    lv = int(step[4:])
                    c = 0 if lv <= JOINS_C else 1
                    if lv == 1:
                        ready("res_raw")
                    if lv == JOINS_C + 1:
                        wait_on(pe, "s1_raw", g)
                    ready(f"xinvT{lv - 1}_ready")
                    ready(f"p{lv}_ready")
                    for t in range(TILES):
                        last = mm(packed((psC, psD)[c][1], lv)[:, t], pn[c][:, t, :],
                                  blocks(xinvT[par], lv, 1)[:, t], start=True, stop=True)
                    last.then_inc(S[f"join{lv}_ps"], 1)
                elif step == "turn":
                    ready(f"xinvT{LEVELS - 2}_ready")
                    pe.sem_inc(apart, 1)
                    for t in range(TILES):
                        last = tr(packed(psD[0], LEVELS - 1)[:, t, 0], xinvT[par][0:P // 2, t, :],
                                  ident[0:P // 2, 0:P // 2])
                    last.then_inc(S["xt_ps"], 1)
                elif step == "u1":
                    ready(f"xinvT{LEVELS - 1}_ready")
                    ready("res_ready")
                    for t in (0, 2):
                        last = mm(psD[0][:, col(t)], xinvT[par][:, t, :], res[par][:, t, :], start=True, stop=True)
                    last.then_inc(S["u1_ps"], 1)
                elif step == "cross":
                    ready("u1_ready")
                    ready("cross_ready")
                    for s in range(2):
                        last = mm(psD[1][:, col(s)], crossT[par][:, 2 * s, :], upd[:, 2 * s, :],
                                  start=True, stop=True)
                    last.then_inc(S["res2_ps"], 1)
                elif step == "u2":
                    ready("res2_ready")
                    for s in range(2):
                        last = mm(psD[0][:, col(s)], xinvT[par][:, 2 * s + 1, :], res2[:, s, :],
                                  start=True, stop=True)
                    last.then_inc(S["u2_ps"], 1)
                elif step == "out":
                    ready("u2_ready")
                    ready("qk_ready")
                    for t in range(TILES):
                        o = psD[1][:, col(t)]
                        mm(o, xT[:, col(t)], m_out[:, :], start=True, stop=False)
                        if t % 2:
                            mm(o, crossT[par][:, t, :], upd[:, t - 1, :], start=False, stop=False)
                        last = mm(o, qkT[par][:, t, :], upd[:, t, :], start=False, stop=True)
                    last.then_inc(S["o_ps"], 1)

            def turn(u):
                pe.wait_ge(S["xu_ready"], u + 1)
                for a in range(HALVES):
                    last = tr(psX[:, a * P:(a + 1) * P], xu[:, a, :], ident[:, :])
                last.then_inc(S["xuT_ps"], 1)

            def hid(u, e):
                pe.wait_ge(S["xuT_ready"], u + 1)
                for j in range(JF):
                    if j % 2 == 0:
                        wait_on(pe, "gelu_ready", (u - 1) * JF + j + 2)
                    last = mm(psH[j // 2][:, (j % 2) * UNIT:(j % 2 + 1) * UNIT],
                              w1_all[:, e, j * P:(j + 1) * P], xuT[:, :], start=True, stop=True)
                    if j % 2:
                        last.then_inc(S["hid_ps"], 1)
                turn(u + 1)

            def out(u, f, e):
                wait_on(pe, "yb_ready", u)
                for k in range(JF):
                    wait_on(pe, "gelu_ready", u * JF + k + 1)
                    for a in range(HALVES):
                        last = mm(psY[a][:, 0:D], h1T[:, k, a * P:(a + 1) * P],
                                  w2_all[:, f * JF + k, :], start=(k == 0), stop=(k == JF - 1))
                    last.then_inc(S["h1_free"], 1)

            def unit_work(what, k=0):
                if what == "first":
                    pe.wait_ge(w_l1, 32)
                    turn(0)
                elif what == "hid":
                    load_bounds(BOUNDS_BY[k])
                    hid(k, k)
                elif what == "out":
                    out(k, k, None)

            bounds = []
            BOUNDS_BY = [min(2 * (k + 1), E + 1) for k in range(E)]

            def load_bounds(upto):
                if len(bounds) < upto:
                    bounds.extend(unit_bounds(pe, len(bounds), upto))

            first_pass(pe, work, unit_work)
            other_units(pe, bounds, hid, out)

        @block.scalar
        def _(act):
            load_small(act)
            f = nc.scalar.activation
            act.wait_ge(prep_ps, 1)
            for n, w in enumerate((wqT, wkT, woutT, tkT)):
                last = f(w[:, :], psA[0][:, n * P:(n + 1) * P], ACT.Copy)
            last.then_inc(prep_sb, 1)
            act.wait_ge(prep_ps, 2)
            for n, w in enumerate((tqT, tvT, w0T)):
                f(w[:, :], psA[1][:, n * P:(n + 1) * P], ACT.Copy)
            f(b1T[:, :], psA[1][:, 3 * P:3 * P + HT + J0], ACT.Copy).then_inc(prep_sb, 1)
            act.wait_ge(prep_ps, 3)
            f(bias_rows[:, :, :], psB[0][:, 0:2 * D].rearrange("p (a d) -> p a d", a=2),
              ACT.Copy).then_inc(prep_sb, 1)
            act.wait_ge(prep_sb, 3)
            f(cb0[:, :], bias_rows[:, 1, :], ACT.Copy, scale=RATE).then_inc(prep_sb, 1)
            act.wait_ge(prep_ps, 4)
            for n in range(2):
                f(b2_all[:, n * E // 2:(n + 1) * E // 2, :], tiles(psC[n]), ACT.Copy)
            f(wvo[:, :], psB[1][:, 0:P], ACT.Copy)
            f(m_out[:, :], psB[1][:, 2 * P:3 * P], ACT.Copy).then_inc(prep_dve, 1)

            act.sem_inc(S["gelu_ready"], SEEDED["gelu_ready"])
            act.sem_inc(S["s0_raw"], SEEDED["s0_raw"])
            act.sem_inc(S["s1_raw"], SEEDED["s1_raw"])

            def work(step, g, par):
                def ready(name, per=1, k=1):
                    wait_on(act, name, g * per + k)

                if step == "xt0":
                    ready("xt0_ps")
                    f(xnT0[par][:, :], psA[0][:, :], ACT.Copy).then_inc(S["xt0_ready"], 1)
                elif step == "v":
                    ready("v0_ps")
                    f(v0[:, :, 0:D], tiles(psA[1]), ACT.Copy).then_inc(S["v0_ready"], 1)
                elif step == "kv":
                    ready("kv0_ps")
                    f(kv0[:, :, :], psA[1][:, :].rearrange("p (s d) -> p s d", s=2)[:, :, 0:D + 1],
                      ACT.Copy).then_inc(S["kv0_ready"], 1)
                elif step in ("lg0", "lg1"):
                    b = int(step[2:])
                    ready(f"d{b}_ready")
                    f(gates[b]["th_lg"][:, :, :], gates[b]["d_lg"][:, :, :], ACT.Tanh,
                      scale=0.5).then_inc(S[f"tanh{b}_ready"], 1)
                elif step == "selT":
                    ready("selT_ps")
                    f(selT[par][:, :], psA[0][0:E, :], ACT.Copy)
                    f(selT_b[par][:, :], psA[0][0:E, :], ACT.Copy).then_inc(S["selTb_ready"], 1)
                elif step == "att":
                    ready("z0_ready")
                    for t in range(TILES):
                        last = f(s0[par][:, t, :], psA[t // 2][:, (t % 2) * 256:(t % 2) * 256 + D],
                                 ACT.Copy, scale=z0[:, t:t + 1])
                    last.then_inc(S["s0_raw"], 1)
                elif step.startswith("hid0"):
                    j = int(step[4:])
                    ready("hid0_ps", J0, j + 1)
                    f(h0T[:, j, :], psB[0][:, :], ACT.Gelu,
                      bias=b1T[:, HT + j:HT + j + 1]).then_inc(S["gelu0_ready"], 1)
                elif step == "y0":
                    ready("y0_ps")
                    for t in range(TILES):
                        last = f(gg0[:, t, :], psB[0][:, t * P:(t + 1) * P], ACT.Copy,
                                 scale=tok_w[par][:, t:t + 1])
                    last.then_inc(S["gg0_ready"], 1)
                elif step == "mix0":
                    ready("gg0_ready")
                    f(th0[:, :, :], gg0[:, :, :], ACT.Tanh, scale=0.5).then_inc(S["silu0_ready"], 1)
                elif step == "xt1":
                    ready("xt1_ps")
                    f(xnT1[par][:, :], psB[1][:, :], ACT.Copy).then_inc(S["xt1_ready"], 1)
                elif step == "kT":
                    ready("kT_ps")
                    f(kT[:, :], psC[0][:, :], ACT.Copy).then_inc(S["kT_ready"], 1)
                elif step == "qT":
                    ready("qT_ps")
                    f(qT[:, :], psC[1][:, :], ACT.Copy).then_inc(S["qT_ready"], 1)
                elif step == "gram_q":
                    ready("one_ready")
                    ready("qk_ps")
                    f(raw[0][:, :, :], tiles(psC[1]), ACT.Copy, bias=1.0).then_inc(S["qk_raw"], 1)
                elif step == "gram_x":
                    ready("cross_ps")
                    f(raw[1][:, :, :], tiles(psC[0]), ACT.Copy, bias=1.0).then_inc(S["cross_raw"], 1)
                elif step == "resid":
                    ready("res_ps")
                    f(res[par][:, :, :], tiles(psC[1]), ACT.Copy).then_inc(S["res_raw"], 1)
                elif step.startswith("half"):
                    lv = int(step[4:])
                    c = 0 if lv <= JOINS_C else 1
                    ready(f"p{lv}_ps")
                    f(blocks(pn[c], lv, 0), packed((psC, psD)[c][0], lv),
                      ACT.Copy).then_inc(S[f"p{lv}_ready"], 1)
                elif step == "turn":
                    ready("xt_ps")
                    f(blocks(xinv[par], LEVELS - 1, 0), packed(psD[0], LEVELS - 1),
                      ACT.Copy).then_inc(S[f"xinv{LEVELS - 2}_ready"], 1)
                elif step == "u1":
                    ready("u1_ps")
                    f(upd[:, 0::2, :], tiles(psD[0])[:, 0::2, :], ACT.Copy).then_inc(S["u1_ready"], 1)
                elif step == "u2":
                    ready("u2_ps")
                    f(upd[:, 1::2, :], tiles(psD[0])[:, 0:2, :], ACT.Copy).then_inc(S["u2_ready"], 1)
                elif step == "out":
                    ready("o_ps")
                    act.sem_inc(apart, 1)
                    f(s1[:, bass.ds(g * TILES, TILES), :], tiles(psD[1]),
                      ACT.Copy).then_inc(S["s1_raw"], 1)

            def turned(u):
                act.wait_ge(S["xuT_ps"], u + 1)
                f(xuT[:, :], psX[:, 0:UNIT], ACT.Copy).then_inc(S["xuT_ready"], 1)

            def gelus(u, e):
                for j in range(JF):
                    n = e * JF + j
                    if j % 2 == 0:
                        act.wait_ge(S["hid_ps"], u * (JF // 2) + j // 2 + 1)
                    wait_on(act, "h1_free", (u - 1) * JF + j + 1)
                    f(h1T[:, j, :], psH[j // 2][:, (j % 2) * UNIT:(j % 2 + 1) * UNIT], ACT.Gelu,
                      bias=b1T[:, n:n + 1]).then_inc(S["gelu_ready"], 1)

            def out(u, f, e):
                if e is not None:
                    gelus(u + 1, e)

            def unit_work(what, k=0):
                if what == "first":
                    turned(0)
                elif what == "hid":
                    turned(k + 1)
                elif what == "gelu":
                    gelus(0, 0)
                elif what == "out":
                    gelus(k + 1, k + 1)
                    if k == 2:
                        bounds.extend(unit_bounds(act))

            bounds = []
            first_pass(act, work, unit_work)
            other_units(act, bounds, lambda u, e: turned(u + 1), out)

            for g in range(groups):
                act.wait_ge(S["sum_ready"], g + 1)
                if g >= 2:
                    act.wait_ge(S["x2_ready"], g - 1)
                f(th1[g % 2][:, :, :], res_c[0][:, g * TILES:(g + 1) * TILES, :], ACT.Tanh,
                  scale=0.5).then_inc(S["silu1_ready"], 1)

        @block.vector
        def _(dve):
            v = nc.vector
            links = dict.fromkeys("ABC", 0)
            counted = [0]

            def then(ins):
                ins.then_inc(count_order, 1)
                counted[0] += 1
                dve.wait_ge(count_order, counted[0])

            CHAIN = {"A": CHAIN_A, "B": CHAIN_B, "C": CHAIN_C}

            def wait_apart(value, *signals):
                for s in signals:
                    dve.wait_ge(S[s], value)
                dve.sem_inc(apart, 1)

            def bc(ap):
                return ap.unsqueeze(2).broadcast_to([P, TILES, E])

            def weight_products():
                dve.wait_ge(prep_dve, 1)
                v.tensor_tensor(m_res[:, :], tvT[:, :], psB[1][:, P:2 * P], ALU.subtract).then_inc(prep_dve, 1)
                dve.wait_ge(prep_dve, 2)
                v.tensor_scalar(m_res[:, :], m_res[:, :], RATE, None, ALU.mult).then_inc(prep_sb, 1)
                dve.wait_ge(consts, 2)
                dve.sem_inc(S["lg1_read"], SEEDED["lg1_read"])
                dve.sem_inc(S[f"xinvT{JOINS_C}_ready"], SEEDED[f"xinvT{JOINS_C}_ready"])
                dve.sem_inc(S["yb_ready"], SEEDED["yb_ready"])
                dve.sem_inc(S["ring_free"], SEEDED["ring_free"])
                dve.sem_inc(S["yw_ready"], SEEDED["yw_ready"])
                v.tensor_copy(filled[:, :], region0[:, :]).then_inc(prep_dve, 1)
                dve.wait_ge(prep_dve, 3)

            def layer_norm(b, h, link, to):
                for t in range(TILES):
                    last = v.bn_stats(stats[b][:, t, :], x_all[:, bass.ds(h * TILES + t, 1), :])
                last.then_inc(S[f"stats{b}_ready"], 1)
                wait_apart(h + 1, f"stats{b}_ready")
                for t in range(TILES):
                    last = v.bn_aggr(mv[b][:, t, :], stats[b][:, t, :])
                link(last)
                r, a = rstd[b][:, :], nt_a[b][:, :]
                link(v.tensor_scalar(v4[b][:, :], mv[b][:, :, 1], LN_EPS, None, ALU.add))
                link(v.tensor_scalar(seed[b][:, :], v4[b][:, :].bitcast(I32), 1, None,
                                     ALU.logical_shift_right))
                link(v.tensor_scalar(r.bitcast(I32), seed[b][:, :], -1.0, float(RSQRT_SEED),
                                     ALU.mult, ALU.add))
                for _ in range(NEWTON):
                    link(v.scalar_tensor_tensor(a, r, -0.5, r, ALU.mult, ALU.mult))
                    link(v.tensor_tensor(a, a, v4[b][:, :], ALU.mult))
                    link(v.scalar_tensor_tensor(r, a, 1.5, r, ALU.add, ALU.mult))
                if b == 1:
                    wait_on(dve, "rows_landed", h - 1)
                for t in range(TILES):
                    last = v.tensor_scalar(to[:, t:t + 1, 0:D], x_all[:, bass.ds(h * TILES + t, 1), :],
                                           mv[b][:, t, 0:1], rstd[b][:, t:t + 1], ALU.subtract, ALU.mult)
                last.then_inc(S[f"xn{b}_ready"], 1)

            def shifted(b, ps, link, h):
                G = gates[b]
                lg = ps[:, 0:TILES * E].rearrange("p (t e) -> p t e", e=E)
                d = G["d_lg"][:, :, :]
                link(v.tensor_reduce(G["m4"][:, :], lg, AX.X, ALU.max))
                v.tensor_tensor(d, lg, bc(G["m4"][:, :]), ALU.subtract).then_inc(S[f"lg{b}_read"], 1)
                wait_on(dve, f"lg{b}_read", h + 1)
                v.tensor_scalar(d, d, EXP_FLOOR, None, ALU.max).then_inc(S[f"d{b}_ready"], 1)

            def two_largest(b, link, h):
                G = gates[b]
                d, tie, first, d2 = (G[n][:, :, :] for n in ("d_lg", "tie", "first", "d2"))
                wait_on(dve, f"d{b}_ready", h + 1)
                link(v.scalar_tensor_tensor(tie, d, 0.0, rank_w[:, :, :], ALU.is_equal, ALU.mult))
                link(v.tensor_reduce(G["r4"][:, :], tie, AX.X, ALU.max))
                link(v.tensor_tensor(first, tie, bc(G["r4"][:, :]), ALU.is_equal))
                link(v.scalar_tensor_tensor(d2, first, -1e30, d, ALU.mult, ALU.add))
                link(v.tensor_reduce(G["m4"][:, :], d2, AX.X, ALU.max))
                link(v.tensor_tensor(tie, d2, bc(G["m4"][:, :]), ALU.is_equal))
                link(v.tensor_tensor(tie, tie, rank_w[:, :, :], ALU.mult))
                link(v.tensor_reduce(G["r4"][:, :], tie, AX.X, ALU.max))
                link(v.tensor_tensor(tie, tie, bc(G["r4"][:, :]), ALU.is_equal))
                v.tensor_tensor(G["sel"][:, :, :], first, tie, ALU.add).then_inc(S[f"sel{b}_ready"], 1)

            def softmax(b, link, h):
                G = gates[b]
                th, num, den, ex = (G[n][:, :, :] for n in ("th_lg", "num", "den", "ex"))
                wait_on(dve, f"tanh{b}_ready", h + 1)
                v.tensor_scalar(num, th, 1.0, None, ALU.add)
                link(v.tensor_scalar(den, th, -1.0, 1.0, ALU.mult, ALU.add))
                link(v.reciprocal(den, den))
                link(v.tensor_tensor(ex, num, den, ALU.mult))
                link(v.tensor_reduce(G["z4"][:, :], ex, AX.X, ALU.add))
                link(v.reciprocal(G["z4"][:, :], G["z4"][:, :]))

            def work(step, g, par):
                def ready(name, per=1, k=1):
                    wait_on(dve, name, g * per + k)

                def link_in(stage):
                    def link(ins):
                        ins.then_inc(order[stage], 1)
                        links[stage] += 1
                        dve.wait_ge(order[stage], g * CHAIN[stage] + links[stage])
                    return link

                def four(m):
                    return m.unsqueeze(1).broadcast_to([P, TILES, P])

                def odd_mask(lv):
                    return blocks(four(mask_lv[:, lv, :].bitcast(I32)), lv, 1)

                in_a, in_b, in_c = link_in("A"), link_in("B"), link_in("C")
                if step == "ln0":
                    links["A"] = 0
                    if isinstance(g, int) and g == 1:
                        dve.wait_ge(x_in[1], 16)
                    layer_norm(0, g, in_a, xn)
                    if isinstance(g, int) and g == 0:
                        weight_products()
                elif step == "lg0":
                    ready("lg0_ps")
                    shifted(0, psA[1], in_a, g)
                elif step == "sel0":
                    two_largest(0, in_a, g)
                elif step == "tok0":
                    softmax(0, in_a, g)
                    G = gates[0]
                    ready("sel0_ready")
                    in_a(v.tensor_tensor(G["ex"][:, :, :], G["ex"][:, :, :], G["sel"][:, :, :], ALU.mult))
                    in_a(v.tensor_reduce(G["m4"][:, :], G["ex"][:, :, :], AX.X, ALU.add))
                    v.tensor_tensor(tok_w[par][:, :], G["m4"][:, :], G["z4"][:, :],
                                    ALU.mult).then_inc(S["sel_ready"], 1)
                elif step == "k":
                    ready("k0_ps")
                    v.tensor_scalar(k0[:, :, :], tiles(psA[0]), 0.0, ATT_EPS, ALU.max,
                                    ALU.add).then_inc(S["k0_ready"], 1)
                elif step == "q":
                    ready("q0_ps")
                    v.tensor_scalar(q0T[:, :], psA[0][:, :], 0.0, ATT_EPS, ALU.max,
                                    ALU.add).then_inc(S["q0_ready"], 1)
                elif step == "att":
                    ready("att_ps")
                    for s in range(2):
                        last = v.tensor_scalar(z0[:, 2 * s:2 * s + 2], psA[s][:, D::256], ATT_EPS, None,
                                               ALU.add)
                    in_a(last)
                    v.reciprocal(z0[:, :], z0[:, :]).then_inc(S["z0_ready"], 1)
                    assert links["A"] == CHAIN_A, links
                elif step.startswith("hid0"):
                    j = int(step[4:])
                    ready("gelu0_ready", J0, j + 1)
                    ready("selb_ps", J0, j + 1)
                    v.tensor_tensor(hg0T[:, j, :], h0T[:, j, :], psB[1][:, :],
                                    ALU.mult).then_inc(S["hg0_ready"], 1)
                elif step == "mix0":
                    links["B"] = 0
                    ready("s0_ready")
                    ready("gg0_ready")
                    in_b(v.tensor_tensor(mix[:, :, :], s0[par][:, :, :], gg0[:, :, :], ALU.mult))
                    ready("silu0_ready")
                    in_b(v.scalar_tensor_tensor(mix[:, :, :], th0[:, :, :], 1.0, mix[:, :, :],
                                                ALU.add, ALU.mult))
                    xg = x_all[:, bass.ds(g * TILES, TILES), :]
                    v.scalar_tensor_tensor(xg, mix[:, :, :], 0.5, xg, ALU.mult,
                                           ALU.add).then_inc(S["x1_ready"], 1)
                elif step == "ln1":
                    wait_apart(g + 1, "x1_ready")
                    layer_norm(1, g, in_b, send[par][0])
                elif step == "lg1":
                    ready("lg1_ps")
                    shifted(1, psB[0], in_b, g)
                    assert links["B"] == CHAIN_B, links
                elif step == "sel1":
                    links["C"] = 0
                    two_largest(1, in_c, g)
                elif step == "pw1":
                    softmax(1, in_c, g)
                    G = gates[1]
                    ex, m4 = G["ex"][:, :, :], G["m4"][:, :]
                    in_c(v.tensor_tensor(ex, ex, bc(G["z4"][:, :]), ALU.mult))
                    ready("sel1_ready")
                    v.tensor_copy(sel_b[:, :].rearrange("p (t e) -> p t e", e=E), G["sel"][:, :, :])
                    in_c(v.tensor_tensor(ex, ex, G["sel"][:, :, :], ALU.mult))
                    in_c(v.tensor_reduce(m4, ex, AX.X, ALU.add))
                    in_c(v.tensor_scalar(m4, m4, NORM_EPS, None, ALU.add))
                    in_c(v.reciprocal(m4, m4))
                    v.tensor_tensor(pw[:, :, :], ex, bc(m4), ALU.mult).then_inc(S["pw_ready"], 1)
                    ready("pw_ready")
                    v.tensor_tensor(pick[:, 0], G["first"][:, :, :], pw[:, :, :], ALU.mult)
                    in_c(v.tensor_tensor(pick[:, 1], G["tie"][:, :, :], pw[:, :, :], ALU.mult))
                    for c in range(CHOICES):
                        v.tensor_reduce(send[par][c][:, :, COL_W], pick[:, c], AX.X, ALU.add)
                elif step == "rank":
                    G = gates[1]
                    ready("rank_ps")
                    in_c(v.tensor_tensor(place[:, :, :],
                                         psB[1][:, 0:TILES * E].rearrange("p (t e) -> p t e", e=E),
                                         filled[:, :].unsqueeze(1).broadcast_to([P, TILES, E]), ALU.add))
                    in_c(v.tensor_tensor(filled[:, :], filled[:, :],
                                         psB[1][:, TILES * E:TILES * E + E], ALU.add))
                    v.tensor_tensor(pick[:, 2], G["first"][:, :, :], place[:, :, :], ALU.mult)
                    in_c(v.tensor_tensor(pick[:, 3], G["tie"][:, :, :], place[:, :, :], ALU.mult))
                    for c in range(CHOICES):
                        last = v.tensor_reduce(slot_f[:, c, :], pick[:, 2 + c], AX.X, ALU.add)
                    in_c(last)
                    v.tensor_copy(slot[par][:, :, :], slot_f[:, :, :]).then_inc(S["slots_ready"], 1)
                    assert links["C"] == CHAIN_C, links
                    if isinstance(g, int) and g == groups - 1:
                        make_table()
                elif step == "gram_n":
                    ready("n_ps")
                    v.scalar_tensor_tensor(nT[par][:, :, :], tiles(psC[0]), 1.0, four(mask_n[:, :]),
                                           ALU.add, ALU.mult).then_inc(S["n_ready"], 1)
                    wait_apart(g + 1, "one_ready", "n_ready")
                    v.copy_predicated(blocks(xinvT[par], 0, 1), odd_mask(0),
                                      blocks(nT[par], 0, 1)).then_inc(S["xinvT0_ready"], 1)
                    ready("xinvT0_ready")
                    v.transpose(xinv[par][:, :, :], xinvT[par][:, :, :]).then_inc(S["xinv0_ready"], 1)
                elif step.startswith("join"):
                    lv = int(step[4:])
                    wait_apart(g + 1, f"join{lv}_ps")
                    v.copy_predicated(blocks(xinvT[par], lv, 1), odd_mask(lv),
                                      packed((psC if lv <= JOINS_C else psD)[1], lv)
                                      ).then_inc(S[f"xinvT{lv}_ready"], 1)
                    if lv < LEVELS - 2:
                        ready(f"xinvT{lv}_ready")
                        v.transpose(xinv[par][:, :, :], xinvT[par][:, :, :]
                                    ).then_inc(S[f"xinv{lv}_ready"], 1)
                elif step == "cross":
                    ready("res2_ps")
                    v.tensor_tensor(res2[:, :, :], tiles(psD[1])[:, 0:2, :], res[par][:, 1::2, :],
                                    ALU.add).then_inc(S["res2_ready"], 1)

            dve.wait_ge(x_in[0], 16)
            def make_table():
                then(v.tensor_tensor(cnt_f[:, :], filled[0:1, :], region0[0:1, :], ALU.subtract))
                then(v.tensor_scalar(cnt_i[:, :], cnt_f[:, :], float(UNIT - 1), None, ALU.add))
                then(v.tensor_scalar(units_i[:, :], cnt_i[:, :], UNIT.bit_length() - 1, None,
                                     ALU.logical_shift_right))
                then(v.tensor_scalar(cnt_f[:, :], units_i[:, :], float(MIN_UNITS), -1.0, ALU.max, ALU.add))
                then(v.memset(bound_f[:, 0:1], float(E)))
                for e in range(E):
                    then(v.tensor_tensor(bound_f[:, e + 1:e + 2], bound_f[:, e:e + 1],
                                         cnt_f[:, e:e + 1], ALU.add))
                then(v.tensor_scalar(units_i[:, 0:1], bound_f[:, E:E + 1], 1.0, None, ALU.add))
                v.tensor_scalar(table[:, 2 * E + 1:2 * E + 2], units_i[:, 0:1], 1, 1,
                                ALU.logical_shift_right, ALU.logical_shift_left)
                v.tensor_copy(table[:, E + 1:2 * E + 1], filled[0:1, :])
                v.tensor_copy(table[:, 0:E + 1], bound_f[:, :]).then_inc(table_ready, 1)

            def take(u):
                wait_on(dve, "unit_in", u * 16 + 16)
                v.tensor_scalar(xu[:, :, :],
                                ring[:, bass.ds(u % RING, 1), :, 0:D].rearrange("p r a d -> p (r a) d"),
                                1.0, None, ALU.mult).then_inc(S["xu_ready"], 1)

            def take_ahead(u):
                dve.wait_ge(S["xuT_ps"], u + 2)
                take(u + 2)

            def results_of(u, f):
                wait_on(dve, "h1_free", (u + 1) * JF)
                wait_on(dve, "yw_ready", u)
                for a in range(HALVES):
                    last = v.tensor_tensor(yb[:, a, :], psY[a][:, 0:D], b2_all[:, f, :], ALU.add)
                last.then_inc(S["yb_ready"], 1)
                wait_on(dve, "y_landed", u - 1)
                at = ring[:, bass.ds(u % RING, 1), :, :]
                mine = bass.ds(u % 2, 1)
                v.tensor_scalar(y_to[:, mine, :].rearrange("p r a -> p (r a)").unsqueeze(2),
                                at[:, :, :, COL_ID:COL_ID + 1].bitcast(I32)
                                .rearrange("p r a d -> p (r a) d"), 0.0, None, ALU.add)
                v.tensor_scalar(y_wt[:, :].unsqueeze(2), at[:, :, :, COL_W:COL_W + 1]
                                .rearrange("p r a d -> p (r a) d"), 1.0, None,
                                ALU.mult).then_inc(S["ring_free"], 1)
                wait_on(dve, "ring_free", u + 1)
                wait_on(dve, "yb_ready", u + 1)
                for a in range(HALVES):
                    last = v.tensor_scalar(yw[:, mine, a, :], yb[:, a:a + 1, :], y_wt[:, a:a + 1],
                                           None, ALU.mult)
                last.then_inc(S["yw_ready"], 1)

            def unit_work(what, k=0):
                if what == "first":
                    take(0)
                    dve.wait_ge(S["xuT_ps"], 1)
                    take(1)
                elif what == "hid":
                    take_ahead(k)
                elif what == "out":
                    results_of(k, k)
                    if k == 2:
                        bounds.extend(unit_bounds(dve))

            bounds = []
            first_pass(dve, work, unit_work)
            other_units(dve, bounds, lambda u, e: take_ahead(u), lambda u, f, e: results_of(u, f))
            wait_on(dve, "yw_ready", bounds[E])
            dve.sem_inc(S["yw_ready"], 1)

            def finish(g):
                ts = slice(g * TILES, (g + 1) * TILES)
                m = mix2[g % 2][:, :, :]
                dve.wait_ge(S["mix_ready"], g + 1)
                dve.wait_ge(S["silu1_ready"], g + 1)
                v.scalar_tensor_tensor(m, th1[g % 2][:, :, :], 1.0, m, ALU.add,
                                       ALU.mult).then_inc(count_order, 1)
                dve.wait_ge(count_order, counted[0] + g + 1)
                v.scalar_tensor_tensor(x_all[:, ts, :], m, 0.5, x_all[:, ts, :], ALU.mult,
                                       ALU.add).then_inc(S["x2_ready"], 1)

            for g in range(groups):
                ts = slice(g * TILES, (g + 1) * TILES)
                dve.wait_ge(res_in[g], 16 * CHOICES)
                v.tensor_tensor(res_c[0][:, ts, :], res_c[0][:, ts, :], res_c[1][:, ts, :],
                                ALU.add).then_inc(S["sum_ready"], 1)
                if g:
                    finish(g - 1)
            finish(groups - 1)


_INS = ['L0_attn_x', 'L0_attn_W_qkv', 'L0_attn_W_out', 'L0_attn_b_out', 'L0_ffn_gate_w', 'L0_ffn_w1',
        'L0_ffn_b1', 'L0_ffn_w2', 'L0_ffn_b2', 'L1_attn_theta_K', 'L1_attn_theta_V',
        'L1_attn_theta_Q', 'L1_attn_W0', 'L1_attn_b0', 'L1_ffn_Wg', 'L1_ffn_W1', 'L1_ffn_b1',
        'L1_ffn_W2', 'L1_ffn_b2']
_OUTS = [((16, 256, 128), 'float32')]


def kernel(**inputs):
    import numpy as _np
    import concourse.bacc as _bacc
    from concourse import mybir as _mybir
    from concourse.bass_utils import run_bass_kernel_spmd as _run

    nc = _bacc.Bacc("TRN2", target_bir_lowering=False, num_devices=1)
    arrays, args = {}, []
    for name in _INS:
        a = _np.ascontiguousarray(inputs[name])
        arrays[f"in_{name}_dram"] = a
        args.append(nc.dram_tensor(f"in_{name}_dram", a.shape, _mybir.dt.from_np(a.dtype), kind="ExternalInput").ap())
    for i, (shape, dtype) in enumerate(_OUTS):
        dt = _mybir.dt.from_np(_np.dtype(dtype))
        args.append(nc.dram_tensor(f"out_{i}_dram", shape, dt, kind="ExternalOutput").ap())
    two_block_kernel(nc, *args)
    r = _run(nc, [arrays], core_ids=[0])
    got = tuple(r.results[0][f"out_{i}_dram"] for i in range(len(_OUTS)))
    return got[0]
```
